# Optimizing a Trainium2 kernel written in Bass

```python
import numpy as np
import jax
import jax.numpy as jnp

def _softmax(x, axis=-1):
    return jax.nn.softmax(x, axis=axis)

def _gelu(x):
    return jax.nn.gelu(x, approximate=True)

def _silu(x):
    return jax.nn.silu(x)

def _sigmoid(x):
    return jax.nn.sigmoid(x)

def _layernorm(x, axis=-1, eps=1e-05):
    m = jnp.mean(x, axis=axis, keepdims=True)
    v = jnp.var(x, axis=axis, keepdims=True)
    return (x - m) / jnp.sqrt(v + eps)

def _scatter_add(tgt, idx, src, axis=0):
    return tgt.at[idx].add(src)

def _segment_sum(src, seg, n):
    return jax.ops.segment_sum(src, seg, n)
kernel_name = 'mk_cond_seq_d1_seqx_r4_0dc797'

def setup_inputs(seed: int=0):
    np.random.seed(seed)
    _w = jnp.asarray

    def _rec_inputs():
        import jax
        import jax.numpy as jnp
        _rk = jax.random.key(seed)
        x = 1.648e-05 + 1 * jax.random.normal(jax.random.fold_in(_rk, 1), (32, 64, 288), jnp.float32)
        _lenS = 64 - jax.random.randint(jax.random.fold_in(_rk, 7), (32,), 0, max(1, 64 // 4) + 1, jnp.int32)
        _lenS2 = 64 - jax.random.randint(jax.random.fold_in(_rk, 8), (32,), 0, max(1, 64 // 4) + 1, jnp.int32)
        cond_1152 = 0.00914911 + 1.00357 * jax.random.normal(jax.random.fold_in(_rk, 11), (32, 288), jnp.float32)
        return (x, cond_1152)
    x, cond_1152 = _rec_inputs()

    def _L0_cond_setup():
        import jax, jax.numpy as jnp
        import numpy as np
        NUM_HEADS = 16
        NUM_EXPERTS = 4
        TOP_K = 2
        LN_EPS = 1e-06

        def _ln(h):
            mu = jnp.mean(h, axis=-1, keepdims=True)
            var = jnp.var(h, axis=-1, keepdims=True)
            return (h - mu) * jax.lax.rsqrt(var + LN_EPS)

        def _modulate(h, shift, scale):
            return h * (1.0 + scale[:, None, :]) + shift[:, None, :]
        key = jax.random.key(seed)
        ks = jax.random.split(key, 12)
        B, N, C = (8, 256, 288)
        H = 4 * C
        E = NUM_EXPERTS
        s = 0.02
        return {'x': jax.random.normal(ks[0], (B, N, C), jnp.float32), 'c': jax.random.normal(ks[1], (B, C), jnp.float32), 'w_adaln': jax.random.normal(ks[2], (C, 6 * C), jnp.float32) * s, 'b_adaln': jnp.zeros((6 * C,), jnp.float32), 'w_qkv': jax.random.normal(ks[3], (C, 3 * C), jnp.float32) * s, 'b_qkv': jnp.zeros((3 * C,), jnp.float32), 'w_proj': jax.random.normal(ks[4], (C, C), jnp.float32) * s, 'b_proj': jnp.zeros((C,), jnp.float32), 'w_gate': jax.random.normal(ks[5], (C, E), jnp.float32) * s, 'w1': jax.random.normal(ks[6], (E, C, H), jnp.float32) * s, 'b1': jnp.zeros((E, H), jnp.float32), 'w2': jax.random.normal(ks[7], (E, H, C), jnp.float32) * s, 'b2': jnp.zeros((E, C), jnp.float32)}
    _L0_cond_all = _L0_cond_setup()
    _L0_cond_in = {k: v for k, v in _L0_cond_all.items() if k in ('w_adaln', 'b_adaln', 'w_qkv', 'b_qkv', 'w_proj', 'b_proj', 'w_gate', 'w1', 'b1', 'w2', 'b2')}
    del _L0_cond_all
    return {'x': x, 'cond_1152': cond_1152, 'L0_cond_w_adaln': _L0_cond_in['w_adaln'], 'L0_cond_b_adaln': _L0_cond_in['b_adaln'], 'L0_cond_w_qkv': _L0_cond_in['w_qkv'], 'L0_cond_b_qkv': _L0_cond_in['b_qkv'], 'L0_cond_w_proj': _L0_cond_in['w_proj'], 'L0_cond_b_proj': _L0_cond_in['b_proj'], 'L0_cond_w_gate': _L0_cond_in['w_gate'], 'L0_cond_w1': _L0_cond_in['w1'], 'L0_cond_b1': _L0_cond_in['b1'], 'L0_cond_w2': _L0_cond_in['w2'], 'L0_cond_b2': _L0_cond_in['b2']}

def reference(x, cond_1152, L0_cond_w_adaln, L0_cond_b_adaln, L0_cond_w_qkv, L0_cond_b_qkv, L0_cond_w_proj, L0_cond_b_proj, L0_cond_w_gate, L0_cond_w1, L0_cond_b1, L0_cond_w2, L0_cond_b2):
    import jax
    import jax.numpy as jnp

    def _L0_cond_ref(x, c, w_adaln, b_adaln, w_qkv, b_qkv, w_proj, b_proj, w_gate, w1, b1, w2, b2):
        import jax, jax.numpy as jnp
        import numpy as np
        NUM_HEADS = 16
        NUM_EXPERTS = 4
        TOP_K = 2
        LN_EPS = 1e-06

        def _ln(h):
            mu = jnp.mean(h, axis=-1, keepdims=True)
            var = jnp.var(h, axis=-1, keepdims=True)
            return (h - mu) * jax.lax.rsqrt(var + LN_EPS)

        def _modulate(h, shift, scale):
            return h * (1.0 + scale[:, None, :]) + shift[:, None, :]
        B, N, C = x.shape
        nh = NUM_HEADS
        hd = C // nh
        mod = jax.nn.silu(c) @ w_adaln + b_adaln
        sh_msa, sc_msa, g_msa, sh_mlp, sc_mlp, g_mlp = jnp.split(mod, 6, axis=-1)
        h = _modulate(_ln(x), sh_msa, sc_msa)
        qkv = (h @ w_qkv + b_qkv).reshape(B, N, 3, nh, hd).transpose(2, 0, 3, 1, 4)
        q, k, v = (qkv[0], qkv[1], qkv[2])
        attn = jax.nn.softmax(jnp.einsum('bhqd,bhkd->bhqk', q, k) * hd ** (-0.5), axis=-1)
        o = jnp.einsum('bhqk,bhkd->bhqd', attn, v).transpose(0, 2, 1, 3).reshape(B, N, C)
        o = o @ w_proj + b_proj
        x = x + g_msa[:, None, :] * o
        xn = _modulate(_ln(x), sh_mlp, sc_mlp)
        xf = xn.reshape(-1, C)
        gate_logits = xf @ w_gate
        topk_logits, topk_idx = jax.lax.top_k(gate_logits, TOP_K)
        gates = jax.nn.softmax(topk_logits, axis=-1)
        cw = jnp.sum(jax.nn.one_hot(topk_idx, NUM_EXPERTS, dtype=xf.dtype) * gates[..., None], axis=1)
        hmid = jax.nn.gelu(jnp.einsum('tc,ech->eth', xf, w1) + b1[:, None, :], approximate=True)
        eo = jnp.einsum('eth,ehc->etc', hmid, w2) + b2[:, None, :]
        moe = jnp.einsum('te,etc->tc', cw, eo).reshape(B, N, C)
        return x + g_mlp[:, None, :] * moe
    x = _L0_cond_ref(x, cond_1152, L0_cond_w_adaln, L0_cond_b_adaln, L0_cond_w_qkv, L0_cond_b_qkv, L0_cond_w_proj, L0_cond_b_proj, L0_cond_w_gate, L0_cond_w1, L0_cond_b1, L0_cond_w2, L0_cond_b2)
    return x

_drawn_inputs = setup_inputs


def setup_inputs(seed=0):
    import zlib

    import numpy as np

    out = dict(_drawn_inputs(seed))
    spreads = {'L0_cond_b_adaln': (0.0, 0.425),
     'L0_cond_b_qkv': (0.0, 0.8),
     'L0_cond_b_proj': (0.0, 0.344),
     'L0_cond_b1': (0.0, 0.8),
     'L0_cond_b2': (0.0, 0.505)}
    factors = {'L0_cond_w_qkv': 7.832,
     'L0_cond_w_proj': 5.242,
     'L0_cond_w_gate': 2.843,
     'L0_cond_w1': 2.678}
    for name, (base, spread) in spreads.items():
        noise = np.random.default_rng([zlib.crc32(name.encode()), seed]).standard_normal(out[name].shape)
        drawn = base * np.exp(spread * noise) if base else spread * noise
        out[name] = jnp.asarray(drawn.astype(out[name].dtype))
    for name, factor in factors.items():
        out[name] = (out[name] * factor).astype(out[name].dtype)
    return out
```

```python
from contextlib import ExitStack

import concourse.bass as bass
from concourse import mybir

FP32 = mybir.dt.float32
FP32R = mybir.dt.float32r
BF16 = mybir.dt.bfloat16
ALU = mybir.AluOpType
ACT = mybir.ActivationFunctionType
AX = mybir.AxisListType

P = 128
PAIRS = [(0, 0), (0, 2), (2, 0), (1, 1), (1, 3), (3, 1), (4, 4)]


def adaln_moe_kernel(nc, x, cond, w_ada, b_ada, w_qkv, b_qkv, w_proj, b_proj, w_gate, w1, b1, w2, b2, out):
    B, N, C = x.shape
    E, _, H = w1.shape
    NH = 16
    HD = C // NH
    T = B * N
    NT = T // P
    TPC = 4
    NC = NT // TPC
    CT = TPC * P
    BPC = CT // N
    KF = C // P
    CR = C - KF * P
    KT = KF + 1
    REP = P // CR
    CX = KT * P
    HG = NH // 4
    HW = 32
    VW = HD + 1
    HJ = H // P
    SCALE = float(HD) ** -0.5
    EPS = 1e-6
    MODN = 6 * C // 4
    SH_A, SC_A, G_A, SH_M, SC_M, G_M = (k * C for k in range(6))
    MODS = (SH_A, SC_A, SH_M, SC_M)

    x_v = x.rearrange("b n c -> (b n) c").rearrange("(i p) c -> p i c", p=P)
    out_v = out.rearrange("b n c -> (b n) c").rearrange("(i p) c -> p i c", p=P)
    gates_dram = nc.dram_tensor("gates_scratch", [B, 2, C], FP32, kind="Internal").ap()
    gates_v = gates_dram.rearrange("(i s) k c -> s k i c", s=P // N)

    ctx = ExitStack()
    with ctx:
        def sb(name, shape, dt=FP32, scope=ctx):
            return scope.enter_context(nc.sbuf_tensor(name, shape, dt))

        def sem(name):
            return ctx.enter_context(nc.semaphore(name))

        ps = ctx.enter_context(nc.psum_tensor("ps", [P, 8, 512], FP32))

        x_sb = sb("x_sb", [P, NT, C])
        xn_all = sb("xn_all", [P, 5, T], FP32R)
        w1_raw = sb("w1_raw", [P, KT, H])
        w2_raw = sb("w2_raw", [P, HJ, C])
        stage_flat = w1_raw[:].rearrange("p k h -> p (k h)")
        assert 4 * C <= H
        wqkv_raw = stage_flat[:, 0:3 * C * KT].rearrange("p (k n) -> p k n", k=KT)
        wp_raw = stage_flat[:, 3 * C * KT:4 * C * KT].rearrange("p (k n) -> p k n", k=KT)
        ident = sb("ident", [P, P])
        logits = sb("logits", [P, NT, E])
        b1_sb = sb("b1_sb", [P, E, HJ])
        minus_half = sb("minus_half", [P, NT])
        tri = sb("tri", [P, E, E])
        r_gt = sb("r_gt", [P, NT, E, E])
        r_eq = sb("r_eq", [P, NT, E, E])
        r_sel = sb("r_sel", [P, NT, E])
        r_exp = sb("r_exp", [P, NT, E])
        r_max = sb("r_max", [P, NT])
        r_sum = sb("r_sum", [P, NT])
        cw = sb("cw", [P, E, NT])

        sa = ExitStack()
        wqk = sb("wqk", [P, 5, 2 * NH, HW], FP32R, sa)
        wv = sb("wv", [P, 5, C], FP32R, sa)
        wp = sb("wp", [P, 5, C], FP32R, sa)
        wg = sb("wg", [P, KT, E], FP32, sa)
        bqk = sb("bqk", [P, 2, HG], FP32, sa)
        bv_b = sb("bv_b", [P, C], FP32, sa)
        bp_b = sb("bp_b", [P, C], FP32, sa)
        modT = sb("modT", [P, 4, KT, B], FP32, sa)
        stats = sb("stats", [P, NT, 6], FP32, sa)
        mv = sb("mv", [P, NT, 2], FP32, sa)
        rstd = sb("rstd", [P, NT], FP32, sa)
        mv2 = sb("mv2", [P, TPC, 2], FP32, sa)
        stats2 = stats[:, 0:TPC, :]
        rstd2 = sb("rstd2", [P, TPC], FP32, sa)
        ybuf = sb("ybuf", [P, TPC, CX], FP32, sa)
        h1 = sb("h1", [P, 5, CT], FP32R, sa)
        h2 = sb("h2", [P, 5, CT], FP32R, sa)
        mtmp = sb("mtmp", [P, 2, CT], FP32, sa)
        gate_sb = sb("gate_sb", [P, TPC, C], FP32, sa)
        va = sb("va", [P, TPC, NH, VW], FP32, sa)
        mpad = sb("mpad", [P, HG, P], FP32, sa)
        rden = sb("rden", [P, NH], FP32, sa)
        o_sb = sb("o_sb", [P, TPC, CX], FP32, sa)
        ox = sb("ox", [P, 2, 5, P], FP32R, sa)
        pj = sb("pj", [P, 2, C], FP32, sa)
        s0 = ExitStack()
        w_ada_sb = sb("w_ada_sb", [P, KT, 6 * C], FP32, s0)
        mod_sb = sb("mod_sb", [B, 6 * C], FP32, s0)
        c_sb = sb("c_sb", [B, 3, C], FP32, s0)
        mod_rest = c_sb[:].rearrange("b k n -> b (k n)")[:, 0:4 * P].rearrange("b (m n) -> b m n", n=P)
        assert 4 * P <= 2 * C
        sT = sb("sT", [P, KT, B], FP32, s0)
        s0.close()
        qT = sb("qT", [P, HG, CT], FP32, sa)
        kT = sb("kT", [P, HG, CT], FP32, sa)
        qTb = sb("qTb", [P, HG, CT], BF16, sa)
        kTb = sb("kTb", [P, HG, CT], BF16, sa)
        pT = sb("pT", [P, 2, 4, HG, N], FP32, sa)
        sa.close()
        w1s = sb("w1s", [P, 5, HJ, P], FP32R)
        w2s = sb("w2s", [P, 2, HJ, C], FP32R)
        hs = sb("hs", [P, 2, HJ, CT], FP32R)
        h32 = sb("h32", [P, 2, CT])
        acc = sb("acc", [P, NT, C])
        yt = sb("yt", [P, 2, C])
        gm = sb("gm", [P, 2, TPC, C])
        b2_b = sb("b2_b", [P, E, C])

        ld_c, ld_ada, ld_x, ld_qkv, ld_wp = map(sem, ("ld_c", "ld_ada", "ld_x", "ld_qkv", "ld_wp"))
        ld_bqk, ld_small, ld_b1, ld_w1, ld_w2 = map(sem, ("ld_bqk", "ld_small", "ld_b1", "ld_w1", "ld_w2"))
        ld_gate, ld_b2, gates_out, xn_copied, stored = map(
            sem, ("ld_gate", "ld_b2", "gates_out", "xn_copied", "stored"))
        ld_gm = [sem("ld_gm0"), sem("ld_gm1")]
        pool_chain, ident_ready, bias_set, consts_ready, pads_ready = map(
            sem, ("pool_chain", "ident_ready", "bias_set", "consts_ready", "pads_ready"))
        wqk_ready, wv_ready, wp_ready, bqk_ready = map(sem, ("wqk_ready", "wv_ready", "wp_ready", "bqk_ready"))
        e_ready, s_ready, sT_done, sT_ready, mod_done, mod_ready, modT_done, modT_ready = map(
            sem, ("e_ready", "s_ready", "sT_done", "sT_ready", "mod_done", "mod_ready", "modT_done", "modT_ready"))
        var1_ready, rstd1_ready = sem("var1_ready"), sem("rstd1_ready")
        dve_chain, passed = sem("dve_chain"), sem("passed")
        y1_ready, t1_done, h1_ready = sem("y1_ready"), sem("t1_done"), sem("h1_ready")
        qk_done, qk_evac, bf_ready, v_done, v_ready = map(sem, ("qk_done", "qk_evac", "bf_ready", "v_done", "v_ready"))
        mx_done, red_done, mt_done, add_done, st_done = map(
            sem, ("mx_done", "red_done", "mt_done", "add_done", "st_done"))
        exp_done, pv_done, o_ready = map(sem, ("exp_done", "pv_done", "o_ready"))
        ot_done, ox_ready, pj_done, pj_evac, x2_ready = map(
            sem, ("ot_done", "ox_ready", "pj_done", "pj_evac", "x2_ready"))
        var2_ready, rstd2_ready, y2_ready, t2_done, h2_ready = map(
            sem, ("var2_ready", "rstd2_ready", "y2_ready", "t2_done", "h2_ready"))
        lg_done, lg_ready, rmax_ready, rexp_ready, cw_ready = map(
            sem, ("lg_done", "lg_ready", "rmax_ready", "rexp_ready", "cw_ready"))
        w1hi, w1_ready, w2hi, w2_ready, acc_zero = map(sem, ("w1hi", "w1_ready", "w2hi", "w2_ready", "acc_zero"))
        s1_done, gelu_done, h_ready, s2_done, s2_evac, res_ready = map(
            sem, ("s1_done", "gelu_done", "h_ready", "s2_done", "s2_evac", "res_ready"))

        block = ctx.enter_context(nc.Block())

        def wait_apart(eng, s, value):
            eng.wait_ge(s, value)
            eng.sem_inc(passed, 1)

        def rows_rep(w):
            return w[KF * P:C, :]

        def load_split(eng, dst, w, s):
            eng.dma_start(dst[:, 0:KF, :], w[0:KF * P, :].rearrange("(k p) n -> p k n", p=P)).then_inc(s, 16)
            for r in range(REP):
                eng.dma_start(dst[CR * r:CR * (r + 1), KF, :], rows_rep(w)).then_inc(s, 16)

        SPLIT_LD = 16 * (REP + 1)

        def rep_last(ap, n):
            return ap[:, KF * P:C].unsqueeze(1).broadcast_to([ap.shape[0], n, CR])

        @block.sync
        def _(sp):
            sp.dma_start(c_sb[:, 0, :], cond).then_inc(ld_c, 16)
            sp.dma_start(w_ada_sb[:, 0:KF, :],
                         w_ada[0:KF * P, :].rearrange("(k p) n -> p k n", p=P)).then_inc(ld_ada, 16)
            sp.dma_start(w_ada_sb[0:CR, KF, :], rows_rep(w_ada)).then_inc(ld_ada, 16)
            sp.dma_start(w_ada_sb[CR:CR + 1, KF, :], b_ada.unsqueeze(0)).then_inc(ld_ada, 16)
            for c in range(NC):
                sp.dma_start(x_sb[:, TPC * c:TPC * (c + 1), :],
                             x_v[:, TPC * c:TPC * (c + 1), :]).then_inc(ld_x, 16)
            sp.wait_ge(mod_ready, 1)
            sp.dma_start(gates_dram[:, 0, :], mod_sb[:, G_A:G_A + C]).then_inc(gates_out, 16)
            sp.dma_start(gates_dram[:, 1, :], mod_sb[:, G_M:G_M + C]).then_inc(gates_out, 16)
            sp.wait_ge(gates_out, 32)
            with sp.Fori(0, NC) as c:
                sp.wait_ge(x2_ready, TPC * c)
                for s in range(P // N):
                    sp.dma_start(gate_sb[N * s:N * (s + 1), :, :],
                                 gates_v[s, 0, bass.ds(TPC * c, TPC), :].partition_broadcast(N)
                                 ).then_inc(ld_gate, 16)
                sp.wait_ge(h2_ready, KT * c + KT)
                sp.dma_start(xn_all[:, :, bass.ds(CT * c, CT)].bitcast(FP32),
                             h2[:, :, :].bitcast(FP32)).then_inc(xn_copied, 16)
            sp.wait_ge(xn_copied, 16 * NC)
            sp.wait_ge(lg_ready, NC)
            for e in range(E):
                sp.dma_start(b2_b[:, e, :], b2[e, :].partition_broadcast(P)).then_inc(ld_b2, 16)
            with sp.Fori(0, E - 1) as e:
                sp.wait_ge(w1_ready, e + 1)
                w1_next = w1[bass.ds(e + 1, 1), :, :].rearrange("a c h -> (a c) h")
                load_split(sp, w1_raw, w1_next, ld_w1)
                sp.wait_ge(w2_ready, e + 1)
                sp.dma_start(w2_raw[:, :, :],
                             w2[bass.ds(e + 1, 1), :, :].rearrange("a (p j) c -> (a p) j c", j=HJ)).then_inc(ld_w2, 16)
            for c in range(NC):
                if c >= 2:
                    sp.wait_ge(res_ready, c - 1)
                for s in range(P // N):
                    sp.dma_start(gm[N * s:N * (s + 1), c % 2, :, :],
                                 gates_v[s, 1, TPC * c:TPC * (c + 1), :].partition_broadcast(N)
                                 ).then_inc(ld_gm[c % 2], 16)
                if c >= 1:
                    sp.wait_ge(res_ready, c)
                    sp.dma_start(out_v[:, TPC * (c - 1):TPC * c, :],
                                 x_sb[:, TPC * (c - 1):TPC * c, :]).then_inc(stored, 16)
            sp.wait_ge(res_ready, NC)
            sp.dma_start(out_v[:, TPC * (NC - 1):NT, :], x_sb[:, TPC * (NC - 1):NT, :]).then_inc(stored, 16)
            sp.wait_ge(stored, 16 * NC)

        @block.gpsimd
        def _(pool):
            nc.gpsimd.memset(ident[:], 0.0).then_inc(pool_chain, 1)
            pool.wait_ge(pool_chain, 1)
            nc.gpsimd.affine_select(out=ident[:], in_=ident[:], compare_op=ALU.not_equal, fill=1.0, base=0,
                                    pattern=[[-1, P]], channel_multiplier=1).then_inc(ident_ready, 1)
            nc.gpsimd.memset(bqk[:, 0, :], 0.0).then_inc(bias_set, 1)
            nc.gpsimd.memset(bqk[:, 1, :], 1.0).then_inc(bias_set, 1)
            nc.gpsimd.memset(wqk[:, 0:3].bitcast(FP32), 0.0).then_inc(pads_ready, 1)
            nc.gpsimd.memset(wqk[:, 3:5].bitcast(FP32), 0.0).then_inc(pads_ready, 1)
            nc.gpsimd.memset(minus_half[:], -0.5).then_inc(pool_chain, 1)
            nc.gpsimd.memset(va[:], 1.0).then_inc(consts_ready, 1)
            nc.gpsimd.memset(mpad[:], 0.0).then_inc(consts_ready, 1)
            nc.gpsimd.memset(wg[:], 0.0).then_inc(bias_set, 1)
            nc.gpsimd.memset(tri[:], 1.0).then_inc(pool_chain, 1)
            pool.wait_ge(pool_chain, 3)
            nc.gpsimd.affine_select(out=tri[:], in_=tri[:], compare_op=ALU.is_gt, fill=0.0, base=0,
                                    pattern=[[1, E], [-1, E]], channel_multiplier=0).then_inc(consts_ready, 1)
            pool.wait_ge(var1_ready, 1)
            nc.gpsimd.tensor_scalar(rstd[:], mv[:, :, 1], EPS, None, ALU.add).then_inc(pool_chain, 1)
            pool.wait_ge(pool_chain, 4)
            nc.gpsimd.tensor_tensor(rstd[:], rstd[:], minus_half[:], ALU.pow).then_inc(rstd1_ready, 1)
            LINKS = TPC + 1
            with pool.Fori(0, NC) as c:
                pool.wait_ge(mx_done, TPC * c)
                wait_apart(pool, qk_evac, 2 * HG * c + HG)

                nc.gpsimd.tensor_copy(qTb[:], qT[:]).then_inc(bf_ready, 1)
                wait_apart(pool, qk_evac, 2 * HG * c + 2 * HG)

                nc.gpsimd.tensor_copy(kTb[:], kT[:]).then_inc(bf_ready, 1)
                pool.wait_ge(ld_gate, 16 * (P // N) * c + 16 * (P // N))
                for i in range(TPC):
                    pool.wait_ge(pj_evac, TPC * c + i + 1)
                    nc.gpsimd.tensor_tensor(pj[:, i % 2, :], pj[:, i % 2, :], gate_sb[:, i, :],
                                            ALU.mult).then_inc(pool_chain, 1)
                    pool.wait_ge(pool_chain, LINKS * c + 4 + i + 1)
                    xt = x_sb[:, bass.ds(TPC * c + i, 1), :].rearrange("p a c -> p (a c)")
                    nc.gpsimd.tensor_tensor(xt, xt, pj[:, i % 2, :], ALU.add).then_inc(x2_ready, 1)
                wait_apart(pool, var2_ready, c + 1)

                nc.gpsimd.tensor_scalar(rstd2[:], mv2[:, :, 1], EPS, None, ALU.add).then_inc(pool_chain, 1)
                pool.wait_ge(pool_chain, LINKS * c + 4 + TPC + 1)
                nc.gpsimd.tensor_tensor(rstd2[:], rstd2[:], minus_half[:, 0:TPC], ALU.pow).then_inc(rstd2_ready, 1)
            pool.wait_ge(lg_ready, NC)
            pool.wait_ge(xn_copied, 16 * NC)
            nc.gpsimd.memset(acc[:], 0.0).then_inc(acc_zero, 1)

        @block.scalar
        def _(act):
            load_split(act, wqkv_raw, w_qkv, ld_qkv)
            act.dma_start(bv_b[:], b_qkv[2 * C:3 * C].partition_broadcast(P)).then_inc(ld_small, 16)
            act.dma_start(bp_b[:], b_proj.partition_broadcast(P)).then_inc(ld_small, 16)
            act.wait_ge(bias_set, 3)
            for qk in range(2):
                for i in range(4):
                    act.dma_start(bqk[HW * i:HW * i + HD, qk, :],
                                  b_qkv[qk * C:(qk + 1) * C].rearrange("(g i d) -> i d g", i=4, d=HD)[i],
                                  allow_slow_non_contiguous=True).then_inc(ld_bqk, 16)
            act.dma_start(wg[:, 0:KF, :], w_gate[0:KF * P, :].rearrange("(k p) n -> p k n", p=P)).then_inc(ld_small, 16)
            for r in (0, 2):
                act.dma_start(wg[CR * r:CR * (r + 1), KF, :], rows_rep(w_gate)).then_inc(ld_small, 16)
            load_split(act, wp_raw, w_proj, ld_wp)
            act.dma_start(b1_sb[:], b1.rearrange("e (p j) -> p e j", j=HJ)).then_inc(ld_b1, 16)
            act.dma_start(w2_raw[:], w2[0].rearrange("(p j) c -> p j c", j=HJ)).then_inc(ld_w2, 16)
            act.wait_ge(ld_c, 16)
            nc.scalar.activation(c_sb[:, 1, :], c_sb[:, 0, :], ACT.Exp, scale=-1.0).then_inc(e_ready, 1)
            act.wait_ge(bqk_ready, 1)
            act.wait_ge(modT_ready, 1)
            act.wait_ge(gates_out, 32)
            act.wait_ge(wv_ready, 1)
            act.wait_ge(wp_ready, 1)
            load_split(act, w1_raw, w1[0], ld_w1)
            with act.Fori(0, NC) as c:
                act.wait_ge(st_done, TPC * c)
                for j in range(2 * HG):
                    act.wait_ge(qk_done, 2 * HG * c + j + 1)
                    dst, scale = (qT, SCALE) if j < HG else (kT, 1.0)
                    nc.scalar.activation(dst[:, j % HG, :], ps[:, 3 + j % 4, :], ACT.Identity,
                                         bias=bqk[:, j // HG, j % HG:j % HG + 1], scale=scale).then_inc(qk_evac, 1)
                for t in range(TPC):
                    act.wait_ge(st_done, TPC * c + t + 1)
                    act.wait_ge(pv_done, TPC * c + max(t - 1, 0))
                    nc.scalar.activation(pT[:, t % 2].rearrange("p i g q -> p i (g q)"), ps[:, 4:8, 0:HG * N],
                                         ACT.Exp).then_inc(exp_done, 1)
            act.wait_ge(rmax_ready, 1)
            nc.scalar.activation(r_exp[:], r_exp[:], ACT.Exp).then_inc(rexp_ready, 1)

            w1_in = w1_raw[:].rearrange("p k (q j) -> p k j q", j=HJ)

            def w1_hi(e):
                act.wait_ge(ld_w1, SPLIT_LD * e + SPLIT_LD)
                act.wait_ge(s1_done, NC * HJ * e)
                for k in range(KT):
                    nc.scalar.activation(w1s[:, 4 if k == KF else k], w1_in[:, k], ACT.Copy).then_inc(w1hi, 1)

            def w2_hi(e):
                act.wait_ge(ld_w2, 16 * e + 16)
                act.wait_ge(s2_done, NT * e)
                nc.scalar.activation(w2s[:, 0], w2_raw[:], ACT.Copy).then_inc(w2hi, 1)

            def expert(e, last):
                w2_hi(e)
                for c in range(NC):
                    for j in range(HJ):
                        n = HJ * c + j
                        act.wait_ge(s1_done, NC * HJ * e + n + 1)
                        wait_apart(act, h_ready, NC * HJ * e + max(n - 1, 0))

                        nc.scalar.activation(h32[:, n % 2, :], ps[:, n % 4, :], ACT.Gelu_apprx_tanh,
                                             bias=b1_sb[:, bass.ds(e, 1), j:j + 1].rearrange("p a b -> p (a b)"),
                                             ).then_inc(gelu_done, 1)
                if not last:
                    w1_hi(e + 1)

            act.wait_ge(ld_b1, 16)
            act.wait_ge(lg_ready, NC)
            act.wait_ge(xn_copied, 16 * NC)
            w1_hi(0)
            with act.Fori(0, E - 1) as e:
                expert(e, False)
            expert(E - 1, True)

        @block.vector
        def _(dve):
            V = nc.vector
            chain = [0, 0]

            def link(ins, base=0):
                chain[0] += 1
                ins.then_inc(dve_chain, 1)
                dve.wait_ge(dve_chain, base + chain[0])

            def split_weight(dst, raw, s):
                for k in range(KF):
                    V.tensor_copy(dst(k), raw(k))
                link(V.tensor_copy(dst(4), raw(KF)))
                for k in range(KF):
                    V.tensor_tensor(dst(2 + k), raw(k), dst(k), ALU.subtract)
                for r in (1, 3):
                    rr = slice(CR * r, CR * (r + 1))
                    last = V.tensor_tensor(dst(4)[rr], raw(KF)[rr], dst(4)[rr], ALU.subtract)
                last.then_inc(s, 1)

            V.memset(sT[CR:CR + 1, KF, :], 1.0).then_inc(ident_ready, 1)
            dve.wait_ge(e_ready, 1)
            link(V.tensor_scalar(c_sb[:, 1, :], c_sb[:, 1, :], 1.0, None, ALU.add))
            link(V.reciprocal(c_sb[:, 2, :], c_sb[:, 1, :]))
            V.tensor_tensor(c_sb[:, 2, :], c_sb[:, 2, :], c_sb[:, 0, :], ALU.mult).then_inc(s_ready, 1)
            dve.wait_ge(ld_qkv, SPLIT_LD)
            dve.wait_ge(pads_ready, 2)
            qk_raw = wqkv_raw[:, :, 0:2 * C].rearrange("p k (h d) -> p k h d", d=HD)
            split_weight(lambda s: wqk[:, s, :, 0:HD], lambda k: qk_raw[:, k], wqk_ready)
            dve.wait_ge(sT_done, 1)
            V.tensor_copy(sT[:, 0:KF, :], ps[:, 0, 0:KF * B].rearrange("p (k b) -> p k b", b=B))
            V.tensor_copy(sT[0:CR, KF, :], ps[0:CR, 0, KF * B:KT * B]).then_inc(sT_ready, 1)
            split_weight(lambda s: wv[:, s, :], lambda k: wqkv_raw[:, k, 2 * C:3 * C], wv_ready)
            dve.wait_ge(mod_done, 1)
            link(V.tensor_copy(mod_sb[:].rearrange("b (g n) -> b g n", n=MODN), ps[0:B, 1:5, 0:MODN]))
            V.tensor_scalar(mod_sb[:, SC_A:SC_A + C], mod_sb[:, SC_A:SC_A + C], 1.0, None, ALU.add)
            link(V.tensor_scalar(mod_sb[:, SC_M:SC_M + C], mod_sb[:, SC_M:SC_M + C], 1.0, None, ALU.add))
            for m, off in enumerate(MODS):
                last = V.tensor_copy(mod_rest[:, m, :].rearrange("b (r n) -> b r n", n=CR),
                                     rep_last(mod_sb[:, off:off + C], REP))
            last.then_inc(mod_ready, 1)
            dve.wait_ge(ld_x, 16 * NC)
            for t in range(NT):
                last = V.bn_stats(stats[:, t, :], x_sb[:, t, :])
            link(last)
            for t in range(NT):
                last = V.bn_aggr(mv[:, t, :], stats[:, t, :])
            last.then_inc(var1_ready, 1)
            dve.wait_ge(modT_done, 1)
            V.tensor_copy(modT[:].rearrange("p m k b -> p (m k b)"), ps[:, 5, 0:4 * KT * B]).then_inc(modT_ready, 1)
            dve.wait_ge(ld_bqk, 8 * 16)
            V.tensor_scalar(bqk[:, 0, :], bqk[:, 0, :], SCALE, None, ALU.mult).then_inc(bqk_ready, 1)
            dve.wait_ge(ld_wp, SPLIT_LD)
            split_weight(lambda s: wp[:, s, :], lambda k: wp_raw[:, k, :], wp_ready)
            dve.wait_ge(rstd1_ready, 1)
            dve.wait_ge(modT_ready, 1)
            dve.wait_ge(consts_ready, 3)
            dve.wait_ge(ld_small, 5 * 16)

            LINKS = 2 * KT * 3 + 3 * TPC + 1
            before = chain[0]
            with dve.Fori(0, NC) as c:
                chain[0] = before
                base = LINKS * c

                def norm(dst, src, mean, r):
                    V.tensor_scalar(dst[:, 0:KF * P], src[:, 0:KF * P], mean, r, ALU.subtract, ALU.mult)
                    return V.tensor_scalar(dst[:, KF * P:CX].rearrange("p (r n) -> p r n", n=CR),
                                           rep_last(src, REP), mean, r, ALU.subtract, ALU.mult)

                def modulate(k, bank, shift, scale, dst, ready):
                    seqs = bass.ds(BPC * c, BPC)
                    tmp = mtmp[:, k % 2, :]
                    tmp3 = tmp.rearrange("p (b n) -> p b n", n=N)

                    def per_seq(kind):
                        return modT[:, kind, k, seqs].unsqueeze(2).broadcast_to([P, BPC, N])
                    link(V.tensor_tensor(tmp3, ps[:, bank, :].rearrange("p (b n) -> p b n", n=N),
                                         per_seq(scale), ALU.mult), base)
                    link(V.tensor_tensor(tmp3, tmp3, per_seq(shift), ALU.add), base)
                    hi = 4 if k == KF else k
                    link(V.tensor_copy(dst[:, hi, :], tmp), base)
                    if k < KF:
                        V.tensor_tensor(dst[:, 2 + k, :], tmp, dst[:, k, :], ALU.subtract).then_inc(ready, 1)
                    else:
                        lo = slice(2 * CR, P)
                        V.tensor_tensor(dst[lo, 4, :], tmp[lo], dst[lo, 4, :], ALU.subtract).then_inc(ready, 1)

                dve.wait_ge(t2_done, KT * c)
                for i in range(TPC):
                    xt = x_sb[:, bass.ds(TPC * c + i, 1), :].rearrange("p a c -> p (a c)")
                    norm(ybuf[:, i, :], xt, mv[:, bass.ds(TPC * c + i, 1), 0:1].rearrange("p a b -> p (a b)"),
                         rstd[:, bass.ds(TPC * c + i, 1)]).then_inc(y1_ready, 1)
                dve.wait_ge(v_done, TPC * c)
                for k in range(KT):
                    dve.wait_ge(t1_done, KT * c + k + 1)
                    modulate(k, k, 0, 1, h1, h1_ready)
                dve.wait_ge(pv_done, TPC * c)
                for i in range(TPC):
                    dve.wait_ge(v_done, TPC * c + i + 1)
                    V.tensor_tensor(va[:, i, :, 0:HD],
                                    ps[:, (7 + i) % 8, 0:C].rearrange("p (h d) -> p h d", d=HD),
                                    bv_b[:].rearrange("p (h d) -> p h d", d=HD), ALU.add).then_inc(v_ready, 1)

                def neg_max(t):
                    dve.wait_ge(mx_done, TPC * c + t + 1)
                    dve.wait_ge(mt_done, TPC * c + t)
                    V.tensor_reduce(
                        mpad[:].rearrange("p g (i w) -> p i g w", w=HW)[:, :, :, HD],
                        ps[:, 0:4, 0:HG * N].rearrange("p i (g k) -> p i g k", k=N),
                        AX.X, ALU.max, negate=True).then_inc(red_done, 1)

                def add_max(t):
                    dve.wait_ge(mt_done, TPC * c + t + 1)
                    q = qT[:, :, P * t:P * (t + 1)]
                    V.tensor_tensor(q, q, ps[:, 0, :].rearrange("p (g q) -> p g q", q=P),
                                    ALU.add).then_inc(add_done, 1)

                def normalise(t):
                    dve.wait_ge(pv_done, TPC * c + t + 1)
                    for s in range(P // N):
                        rows = slice(N * s, N * (s + 1))
                        o_ps = ps[rows, 4 + s, 0:NH * VW].rearrange("p (h d) -> p h d", d=VW)
                        last = V.reciprocal(rden[rows, :], o_ps[:, :, HD])
                    link(last, base)
                    for s in range(P // N):
                        rows = slice(N * s, N * (s + 1))
                        o_ps = ps[rows, 4 + s, 0:NH * VW].rearrange("p (h d) -> p h d", d=VW)
                        last = V.tensor_tensor(o_sb[rows, t, 0:C].rearrange("p (h d) -> p h d", d=HD), o_ps[:, :, 0:HD],
                                               rden[rows, :].unsqueeze(2).broadcast_to([N, NH, HD]), ALU.mult)
                    link(last, base)
                    V.tensor_copy(o_sb[:, t, C:CX].rearrange("p (r n) -> p r n", n=CR),
                                  rep_last(o_sb[:, t, :], REP - 1)).then_inc(o_ready, 1)

                neg_max(0)
                add_max(0)
                for t in range(TPC):
                    if t + 1 < TPC:
                        neg_max(t + 1)
                    normalise(t)
                    if t + 1 < TPC:
                        add_max(t + 1)

                def split_o(i):
                    dve.wait_ge(ot_done, TPC * c + i + 1)
                    if i >= 2:
                        dve.wait_ge(pj_done, TPC * c + i - 1)
                    o = ox[:, i % 2]
                    src = ps[:, i % 2, 0:KT * P].rearrange("p (k t) -> p k t", t=P)
                    V.tensor_copy(o[:, 0:KF, :], src[:, 0:KF, :])
                    link(V.tensor_copy(o[:, 4, :], src[:, KF, :]), base)
                    V.tensor_tensor(o[:, 2:2 + KF, :], src[:, 0:KF, :], o[:, 0:KF, :], ALU.subtract)
                    lo = slice(2 * CR, P)
                    V.tensor_tensor(o[lo, 4, :], src[lo, KF, :], o[lo, 4, :], ALU.subtract).then_inc(ox_ready, 1)

                def projected(i):
                    dve.wait_ge(pj_done, TPC * c + i + 1)
                    if i >= 2:
                        dve.wait_ge(x2_ready, TPC * c + i - 1)
                    V.tensor_tensor(pj[:, i % 2, :], ps[:, 2 + i % 2, 0:C], bp_b[:], ALU.add).then_inc(pj_evac, 1)

                split_o(0)
                for i in range(TPC):
                    if i + 1 < TPC:
                        split_o(i + 1)
                    projected(i)
                for i in range(TPC):
                    wait_apart(dve, x2_ready, TPC * c + i + 1)
                    xt = x_sb[:, bass.ds(TPC * c + i, 1), :].rearrange("p a c -> p (a c)")
                    last = V.bn_stats(stats2[:, i, :], xt)
                link(last, base)
                dve.sem_inc(passed, 1)
                for i in range(TPC):
                    last = V.bn_aggr(mv2[:, i, :], stats2[:, i, :])
                last.then_inc(var2_ready, 1)
                dve.wait_ge(rstd2_ready, c + 1)
                for i in range(TPC):
                    xt = x_sb[:, bass.ds(TPC * c + i, 1), :].rearrange("p a c -> p (a c)")
                    norm(ybuf[:, i, :], xt, mv2[:, i, 0:1], rstd2[:, i:i + 1]).then_inc(y2_ready, 1)
                dve.wait_ge(xn_copied, 16 * c)
                for k in range(KT):
                    dve.wait_ge(t2_done, KT * c + k + 1)
                    modulate(k, 4 + k, 2, 3, h2, h2_ready)
                dve.wait_ge(lg_done, c + 1)
                V.tensor_copy(logits[:, bass.ds(TPC * c, TPC), :],
                              ps[:, 7, 0:TPC * E].rearrange("p (i e) -> p i e", e=E)).then_inc(lg_ready, 1)
                assert chain[0] - before == LINKS, chain[0] - before
            chain[0] = before + LINKS * NC
            dve.wait_ge(lg_ready, NC)

            l_j = logits[:].unsqueeze(2).broadcast_to([P, NT, E, E])
            l_e = logits[:].unsqueeze(3).broadcast_to([P, NT, E, E])
            V.tensor_tensor(r_gt[:], l_j, l_e, ALU.is_gt)
            V.tensor_reduce(r_max[:], logits[:], AX.X, ALU.max)
            link(V.tensor_tensor(r_eq[:], l_j, l_e, ALU.is_equal))
            V.tensor_tensor(r_exp[:], logits[:], r_max[:].unsqueeze(2).broadcast_to([P, NT, E]),
                            ALU.subtract).then_inc(rmax_ready, 1)
            eq16 = r_eq[:].rearrange("p t e j -> p t (e j)")
            tri16 = tri[:].rearrange("p e j -> p (e j)").unsqueeze(1).broadcast_to([P, NT, E * E])
            link(V.tensor_tensor(eq16, eq16, tri16, ALU.mult))
            link(V.tensor_tensor(r_gt[:], r_gt[:], r_eq[:], ALU.add))
            link(V.tensor_reduce(r_sel[:], r_gt[:], AX.X, ALU.add))
            link(V.tensor_scalar(r_sel[:], r_sel[:], 1.5, None, ALU.is_lt))
            dve.wait_ge(rexp_ready, 1)
            link(V.tensor_tensor(r_sel[:], r_sel[:], r_exp[:], ALU.mult))
            link(V.tensor_reduce(r_sum[:], r_sel[:], AX.X, ALU.add))
            link(V.reciprocal(r_sum[:], r_sum[:]))
            V.tensor_tensor(cw[:].rearrange("p e t -> p t e"), r_sel[:],
                            r_sum[:].unsqueeze(2).broadcast_to([P, NT, E]), ALU.mult).then_inc(cw_ready, 1)
            dve.wait_ge(cw_ready, 1)

            w1_in = w1_raw[:].rearrange("p k (q j) -> p k j q", j=HJ)

            def w1_lo(e):
                dve.wait_ge(w1hi, KT * e + KT)
                for k in range(KF):
                    V.tensor_tensor(w1s[:, 2 + k], w1_in[:, k], w1s[:, k], ALU.subtract)
                for r in (1, 3):
                    rr = slice(CR * r, CR * (r + 1))
                    last = V.tensor_tensor(w1s[rr, 4], w1_in[rr, KF], w1s[rr, 4], ALU.subtract)
                last.then_inc(w1_ready, 1)

            def w2_lo(e):
                dve.wait_ge(w2hi, e + 1)
                V.tensor_tensor(w2s[:, 1], w2_raw[:], w2s[:, 0], ALU.subtract).then_inc(w2_ready, 1)

            EL = NC * (HJ + TPC)

            def expert(e, last):
                before = chain[0]
                base = EL * e if not last else 0
                w2_lo(e)
                for c in range(NC):
                    dve.wait_ge(s2_done, NT * e + TPC * c)
                    for j in range(HJ):
                        n = HJ * c + j
                        dve.wait_ge(gelu_done, NC * HJ * e + n + 1)
                        link(V.tensor_copy(hs[:, 0, j, :], h32[:, n % 2, :]), base)
                        V.tensor_tensor(hs[:, 1, j, :], h32[:, n % 2, :], hs[:, 0, j, :],
                                        ALU.subtract).then_inc(h_ready, 1)
                    if c == NC - 1 and not last:
                        w1_lo(e + 1)
                    for i in range(TPC):
                        t = TPC * c + i
                        dve.wait_ge(s2_done, NT * e + t + 1)
                        link(V.tensor_tensor(yt[:, i % 2, :], ps[:, 4 + i, 0:C],
                                             b2_b[:, bass.ds(e, 1), :].rearrange("p a c -> p (a c)"), ALU.add), base)
                        V.scalar_tensor_tensor(acc[:, t, :], yt[:, i % 2, :],
                                               cw[:, bass.ds(e, 1), t:t + 1].rearrange("p a b -> p (a b)"),
                                               acc[:, t, :], ALU.mult, ALU.add).then_inc(s2_evac, 1)
                    if last:
                        tiles = slice(TPC * c, TPC * (c + 1))
                        dve.wait_ge(ld_gm[c % 2], 16 * (P // N) * (c // 2 + 1))
                        dve.wait_ge(s2_evac, NT * e + TPC * (c + 1))
                        link(V.tensor_tensor(gm[:, c % 2], gm[:, c % 2], acc[:, tiles, :], ALU.mult), base)
                        V.tensor_tensor(x_sb[:, tiles, :], x_sb[:, tiles, :], gm[:, c % 2],
                                        ALU.add).then_inc(res_ready, 1)
                return chain[0] - before

            w1_lo(0)
            dve.wait_ge(ld_b2, 16 * E)
            dve.wait_ge(acc_zero, 1)
            with dve.Fori(0, E - 1) as e:
                n = expert(e, False)
                assert n == EL, n
            chain[0] += EL * (E - 2)
            expert(E - 1, True)

        @block.tensor
        def _(pe):
            M = nc.tensor.matmul

            def split_matmul(out_ap, stat, mov):
                for n, (a, b) in enumerate(PAIRS):
                    last = M(out_ap, stat(a), mov(b), start=(n == 0), stop=(n == len(PAIRS) - 1))
                return last

            pe.wait_ge(ident_ready, 2)
            pe.wait_ge(s_ready, 1)
            for k in range(KT):
                n = P if k < KF else CR
                last = nc.tensor.transpose(ps[0:n, 0, B * k:B * (k + 1)], c_sb[:, 2, P * k:P * k + n], ident[0:B, 0:B])
            last.then_inc(sT_done, 1)
            pe.wait_ge(sT_ready, 1)
            pe.wait_ge(ld_ada, 3 * 16)
            for g in range(4):
                cols = slice(MODN * g, MODN * (g + 1))
                o = ps[0:B, 1 + g, 0:MODN]
                for k in range(KT):
                    n = P if k < KF else CR + 1
                    last = M(o, sT[0:n, k, :], w_ada_sb[0:n, k, cols], start=(k == 0), stop=(k == KF))
            last.then_inc(mod_done, 1)
            pe.wait_ge(mod_ready, 1)
            for m, off in enumerate(MODS):
                for k in range(KT):
                    src = mod_sb[:, off + P * k:off + P * (k + 1)] if k < KF else mod_rest[:, m, :]
                    last = nc.tensor.transpose(ps[:, 5, B * (KT * m + k):B * (KT * m + k + 1)], src, ident[0:B, 0:B])
            last.then_inc(modT_done, 1)
            pe.wait_ge(modT_ready, 1)
            pe.wait_ge(wqk_ready, 1)
            pe.wait_ge(wv_ready, 1)
            pe.wait_ge(wp_ready, 1)
            pe.wait_ge(ld_small, 5 * 16)

            def transpose_channels(src, i, out_ap, k):
                return nc.tensor.transpose(out_ap, src[:, i, P * k:P * (k + 1)], ident[:])

            with pe.Fori(0, NC) as c:
                pe.wait_ge(y1_ready, TPC * c + TPC)
                for k in range(KT):
                    for i in range(TPC):
                        last = transpose_channels(ybuf, i, ps[:, k, P * i:P * (i + 1)], k)
                    last.then_inc(t1_done, 1)
                pe.wait_ge(h1_ready, KT * c + KT)
                pe.wait_ge(h2_ready, KT * c)
                for j in range(2 * HG):
                    if j >= 4:
                        pe.wait_ge(qk_evac, 2 * HG * c + j - 3)
                    split_matmul(ps[:, 3 + j % 4, :],
                                 lambda a: wqk[:, a, 4 * j:4 * (j + 1), :].rearrange("p h w -> p (h w)"),
                                 lambda b: h1[:, b, :]).then_inc(qk_done, 1)
                pe.wait_ge(lg_ready, c)
                for i in range(TPC):
                    split_matmul(ps[:, (7 + i) % 8, 0:C], lambda a: h1[:, a, P * i:P * (i + 1)],
                                 lambda b: wv[:, b, :]).then_inc(v_done, 1)

                def heads(t):
                    for s in range(P // N):
                        for g in range(HG):
                            for i in range(4):
                                yield s, g, i, slice(HW * i, HW * (i + 1)), slice(P * t + N * s, P * t + N * (s + 1))

                def max_scores(t):
                    if t:
                        pe.wait_ge(add_done, TPC * c + t)
                    for s, g, i, rows, toks in heads(t):
                        last = M(ps[N * s:N * (s + 1), i, N * g:N * (g + 1)], qTb[rows, g, toks], kTb[rows, g, toks],
                                 start=True, stop=True)
                    last.then_inc(mx_done, 1)

                def move_max(t):
                    pe.wait_ge(red_done, TPC * c + t + 1)
                    for g in range(HG):
                        last = nc.tensor.transpose(ps[:, 0, P * g:P * (g + 1)], mpad[:, g, :], ident[:])
                    last.then_inc(mt_done, 1)

                def scores(t):
                    pe.wait_ge(add_done, TPC * c + t + 1)
                    if t:
                        pe.wait_ge(o_ready, TPC * c + t)
                    for s, g, i, rows, toks in heads(t):
                        last = M(ps[N * s:N * (s + 1), 4 + i, N * g:N * (g + 1)], kT[rows, g, toks], qT[rows, g, toks],
                                 start=True, stop=True)
                    last.then_inc(st_done, 1)

                def weigh_values(t):
                    wait_apart(pe, exp_done, TPC * c + t + 1)

                    for h in range(NH):
                        for s in range(P // N):
                            rows = slice(N * s, N * (s + 1))
                            last = M(ps[rows, 4 + s, VW * h:VW * (h + 1)], pT[rows, t % 2, h % 4, h // 4, :],
                                     va[rows, t, h, :], start=True, stop=True)
                    last.then_inc(pv_done, 1)

                pe.wait_ge(v_ready, TPC * c + TPC)
                pe.wait_ge(qk_evac, 2 * HG * c + 2 * HG)
                pe.wait_ge(bf_ready, 2 * c + 2)
                max_scores(0)
                move_max(0)
                for t in range(TPC):
                    scores(t)
                    if t + 1 < TPC:
                        max_scores(t + 1)
                    weigh_values(t)
                    if t + 1 < TPC:
                        move_max(t + 1)

                def transpose_o(i):
                    pe.wait_ge(o_ready, TPC * c + i + 1)
                    if i >= 2:
                        pe.wait_ge(ox_ready, TPC * c + i - 1)
                    for k in range(KT):
                        last = transpose_channels(o_sb, i, ps[:, i % 2, P * k:P * (k + 1)], k)
                    last.then_inc(ot_done, 1)

                transpose_o(0)
                for i in range(TPC):
                    if i + 1 < TPC:
                        transpose_o(i + 1)
                    pe.wait_ge(ox_ready, TPC * c + i + 1)
                    if i >= 2:
                        pe.wait_ge(pj_evac, TPC * c + i - 1)
                    split_matmul(ps[:, 2 + i % 2, 0:C], lambda a: ox[:, i % 2, a, :],
                                 lambda b: wp[:, b, :]).then_inc(pj_done, 1)
                pe.wait_ge(y2_ready, TPC * c + TPC)
                for k in range(KT):
                    for i in range(TPC):
                        last = transpose_channels(ybuf, i, ps[:, 4 + k, P * i:P * (i + 1)], k)
                    last.then_inc(t2_done, 1)
                pe.wait_ge(h2_ready, KT * c + KT)
                for i in range(TPC):
                    o = ps[:, 7, E * i:E * (i + 1)]
                    for n, (slot, k) in enumerate(((0, 0), (2, 0), (1, 1), (3, 1), (4, 2))):
                        last = M(o, h2[:, slot, P * i:P * (i + 1)].bitcast(FP32), wg[:, k, :],
                                 start=(n == 0), stop=(n == 4))
                last.then_inc(lg_done, 1)

            def expert(e):
                for c in range(NC):
                    if c == 0:
                        pe.wait_ge(w1_ready, e + 1)
                        pe.wait_ge(gelu_done, NC * HJ * e)
                    for j in range(HJ):
                        n = HJ * c + j
                        if n >= 4:
                            pe.wait_ge(gelu_done, NC * HJ * e + n - 3)
                        split_matmul(ps[:, n % 4, :], lambda a: w1s[:, a, j, :],
                                     lambda b: xn_all[:, b, CT * c:CT * (c + 1)]).then_inc(s1_done, 1)
                    if c == 0:
                        pe.wait_ge(w2_ready, e + 1)
                    pe.wait_ge(s2_evac, NT * e + TPC * c)
                    for i in range(TPC):
                        toks = slice(P * i, P * (i + 1))
                        for j in range(HJ):
                            if i == 0:
                                pe.wait_ge(h_ready, NC * HJ * e + HJ * c + j + 1)
                            for n, (a, b) in enumerate(((0, 0), (0, 1), (1, 0))):
                                last = M(ps[:, 4 + i, 0:C], hs[:, a, j, toks], w2s[:, b, j, :],
                                         start=(j == 0 and n == 0), stop=(j == HJ - 1 and n == 2))
                        last.then_inc(s2_done, 1)

            pe.wait_ge(xn_copied, 16 * NC)
            pe.wait_ge(lg_ready, NC)
            with pe.Fori(0, E - 1) as e:
                expert(e)
            expert(E - 1)


_INS = ["x", "cond_1152", "L0_cond_w_adaln", "L0_cond_b_adaln", "L0_cond_w_qkv", "L0_cond_b_qkv", "L0_cond_w_proj",
        "L0_cond_b_proj", "L0_cond_w_gate", "L0_cond_w1", "L0_cond_b1", "L0_cond_w2", "L0_cond_b2"]


def kernel(**inputs):
    import numpy as _np
    import concourse.bacc as _bacc
    from concourse import mybir as _mybir
    from concourse.bass_utils import run_bass_kernel_spmd as _run

    nc = _bacc.Bacc("TRN2", target_bir_lowering=False, num_devices=1)
    arrays, args = {}, []
    for name in _INS:
        a = _np.ascontiguousarray(inputs[name])
        arrays[f"in_{name}_dram"] = a
        args.append(nc.dram_tensor(f"in_{name}_dram", a.shape, _mybir.dt.from_np(a.dtype), kind="ExternalInput").ap())
    out = nc.dram_tensor("out_dram", inputs["x"].shape, _mybir.dt.float32, kind="ExternalOutput").ap()
    adaln_moe_kernel(nc, *args, out)
    r = _run(nc, [arrays], core_ids=[0])
    return r.results[0]["out_dram"]
```

```python
from contextlib import ExitStack

import concourse.bass as bass
from concourse import mybir

FP32 = mybir.dt.float32
FP32R = mybir.dt.float32r
BF16 = mybir.dt.bfloat16
ALU = mybir.AluOpType
ACT = mybir.ActivationFunctionType
AX = mybir.AxisListType

P = 128
PAIRS = [(0, 0), (0, 3), (3, 0), (1, 1), (1, 4), (4, 1), (2, 2)]
REST, LO = 2, 3


def adaln_moe_kernel(nc, x, cond, w_ada, b_ada, w_qkv, b_qkv, w_proj, b_proj, w_gate, w1, b1, w2, b2, out):
    B, N, C = x.shape
    E, _, H = w1.shape
    NH = 16
    HD = C // NH
    T = B * N
    NT = T // P
    TPC = 4
    NC = NT // TPC
    CT = TPC * P
    BPC = CT // N
    KF = C // P
    CR = C - KF * P
    KT = KF + 1
    REP = P // CR
    CX = KT * P
    HG = NH // 4
    HW = 32
    VW = HD + 1
    HJ = H // P
    SCALE = float(HD) ** -0.5
    EPS = 1e-6
    MODN = 6 * C // 4
    SH_A, SC_A, G_A, SH_M, SC_M, G_M = (k * C for k in range(6))

    x_v = x.rearrange("b n c -> (b n) c").rearrange("(i p) c -> p i c", p=P)
    out_v = out.rearrange("b n c -> (b n) c").rearrange("(i p) c -> p i c", p=P)
    SEQS = P // N
    mods_dram = nc.dram_tensor("mods_scratch", [B, 6 * C], FP32, kind="Internal").ap()
    mods_v = mods_dram.rearrange("(i s) c -> s i c", s=SEQS)

    ctx = ExitStack()
    with ctx:
        def sb(name, shape, dt=FP32, scope=ctx):
            return scope.enter_context(nc.sbuf_tensor(name, shape, dt))

        def sem(name):
            return ctx.enter_context(nc.semaphore(name))

        ps = ctx.enter_context(nc.psum_tensor("ps", [P, 8, 512], FP32))

        x_sb = sb("x_sb", [P, NT, C])
        xn_all = sb("xn_all", [P, 5, T], FP32R)
        s_att = ExitStack()
        kblk = sb("kblk", [P, HG, BPC, 4, N], BF16, s_att)
        pT = sb("pT", [P, 4, HG, N], FP32, s_att)
        s_att.close()
        w1_raw = sb("w1_raw", [P, KT, H])
        w2_raw = sb("w2_raw", [P, HJ, C])
        stage_flat = w1_raw[:].rearrange("p k h -> p (k h)")
        assert 4 * C <= H
        wqkv_raw = stage_flat[:, 0:3 * C * KT].rearrange("p (k n) -> p k n", k=KT)
        wp_raw = stage_flat[:, 3 * C * KT:4 * C * KT].rearrange("p (k n) -> p k n", k=KT)
        ident = sb("ident", [P, P])
        logits = sb("logits", [P, NT, E])
        b1_sb = sb("b1_sb", [P, E, HJ])
        minus_half = sb("minus_half", [P, NT])
        tri = sb("tri", [P, E, E])
        r_gt = sb("r_gt", [P, NT, E, E])
        r_eq = sb("r_eq", [P, NT, E, E])
        r_sel = sb("r_sel", [P, NT, E])
        r_exp = sb("r_exp", [P, NT, E])
        r_max = sb("r_max", [P, NT])
        r_sum = sb("r_sum", [P, NT])
        cw = sb("cw", [P, E, NT])

        sa = ExitStack()
        wqk = sb("wqk", [P, 5, 2 * NH, HW], FP32R, sa)
        wv = sb("wv", [P, 5, C], FP32R, sa)
        wp = sb("wp", [P, 5, C], FP32R, sa)
        wg = sb("wg", [P, KT, E], FP32, sa)
        bqk = sb("bqk", [P, 2, HG], FP32, sa)
        bv_b = sb("bv_b", [P, C], FP32, sa)
        bp_b = sb("bp_b", [P, C], FP32, sa)
        stats = sb("stats", [P, NT, 6], FP32, sa)
        mv = sb("mv", [P, NT, 2], FP32, sa)
        rstd = sb("rstd", [P, NT], FP32, sa)
        mv2 = sb("mv2", [P, 2, 2], FP32, sa)
        stats2 = sb("stats2", [P, 2, 6], FP32, sa)
        rstd2 = sb("rstd2", [P, 2], FP32, sa)
        mods1 = sb("mods1", [P, TPC, 2, C], FP32, sa)
        mods2 = sb("mods2", [P, TPC, 3, C], FP32, sa)
        y1 = sb("y1", [P, TPC, CX], FP32, sa)
        y2 = sb("y2", [P, 2, CX], FP32, sa)
        yT = sb("yT", [P, 2, KT, P], FP32, sa)
        h1 = sb("h1", [P, 5, CT], FP32R, sa)
        va = sb("va", [P, TPC, NH, VW], FP32, sa)
        mpad = sb("mpad", [P, HG, P], FP32, sa)
        rden = sb("rden", [P, NH], FP32, sa)
        o_sb = sb("o_sb", [P, 2, CX], FP32, sa)
        ox = sb("ox", [P, 2, 5, P], FP32R, sa)
        pj = sb("pj", [P, 2, C], FP32, sa)
        s0 = ExitStack()
        w_ada_sb = sb("w_ada_sb", [P, KT, 6 * C], FP32, s0)
        assert 9 * C + KT * B <= TPC * 3 * C
        mods2_flat = mods2[:].rearrange("p i k c -> p (i k c)")
        mod_sb = mods2_flat[0:B, 0:6 * C]
        c_sb = mods2_flat[0:B, 6 * C:9 * C].rearrange("b (k c) -> b k c", c=C)
        sT = mods2_flat[:, 9 * C:9 * C + KT * B].rearrange("p (k b) -> p k b", b=B)
        s0.close()
        qT = sb("qT", [P, HG, CT], FP32, sa)
        kT = sb("kT", [P, HG, CT], FP32, sa)
        qTb = sb("qTb", [P, HG, CT], BF16, sa)
        kTb = sb("kTb", [P, HG, CT], BF16, sa)
        sa.close()
        w1s = sb("w1s", [P, 5, HJ, P], FP32R)
        w2s = sb("w2s", [P, 2, HJ, C], FP32R)
        hs = sb("hs", [P, 2, HJ, CT], FP32R)
        h32 = sb("h32", [P, 2, CT])
        acc = sb("acc", [P, NT, C])
        yt = sb("yt", [P, 2, C])
        gm = sb("gm", [P, 2, TPC, C])
        b2_b = sb("b2_b", [P, E, C])

        ld_c, ld_ada, ld_x, ld_qkv, ld_wp = map(sem, ("ld_c", "ld_ada", "ld_x", "ld_qkv", "ld_wp"))
        ld_bqk, ld_small, ld_b1, ld_w1, ld_w2 = map(sem, ("ld_bqk", "ld_small", "ld_b1", "ld_w1", "ld_w2"))
        ld_mods1, ld_mods2, ld_b2, mods_out, stored = map(
            sem, ("ld_mods1", "ld_mods2", "ld_b2", "mods_out", "stored"))
        ld_gm = [sem("ld_gm0"), sem("ld_gm1")]
        pool_chain, ident_ready, bias_set, consts_ready, pads_ready = map(
            sem, ("pool_chain", "ident_ready", "bias_set", "consts_ready", "pads_ready"))
        wqk_ready, wv_ready, wp_ready, bqk_ready = map(sem, ("wqk_ready", "wv_ready", "wp_ready", "bqk_ready"))
        e_ready, s_ready, sT_done, sT_ready, mod_done, mod_ready = map(
            sem, ("e_ready", "s_ready", "sT_done", "sT_ready", "mod_done", "mod_ready"))
        var1_ready, rstd1_ready = sem("var1_ready"), sem("rstd1_ready")
        dve_chain, passed = sem("dve_chain"), sem("passed")
        y1_norm, y1_ready, t1_done, h1_hi, h1_ready = map(sem, ("y1_norm", "y1_ready", "t1_done", "h1_hi", "h1_ready"))
        qk_done, qk_read, kTb_ready, kblk_zero, kblk_ready, v_done, v_ready = map(sem, ("qk_done", "qk_read", "kTb_ready", "kblk_zero", "kblk_ready", "v_done", "v_ready"))
        mx_done, red_done, mt_done, add_done, st_done = map(
            sem, ("mx_done", "red_done", "mt_done", "add_done", "st_done"))
        exp_done, pv_done, o_ready = map(sem, ("exp_done", "pv_done", "o_ready"))
        ot_done, ox_hi, ox_ready, pj_done, pj_read, x2_ready = map(
            sem, ("ot_done", "ox_hi", "ox_ready", "pj_done", "pj_read", "x2_ready"))
        var2_ready, rstd2_ready, y2_norm, y2_ready, t2_done, yT_ready, xn_hi, xn_ready = map(
            sem, ("var2_ready", "rstd2_ready", "y2_norm", "y2_ready", "t2_done", "yT_ready", "xn_hi", "xn_ready"))
        lg_done, lg_ready, rmax_ready, rexp_ready, cw_ready = map(
            sem, ("lg_done", "lg_ready", "rmax_ready", "rexp_ready", "cw_ready"))
        w1hi, w1_ready, w2hi, w2_ready, acc_zero = map(sem, ("w1hi", "w1_ready", "w2hi", "w2_ready", "acc_zero"))
        s1_done, gelu_done, h_ready, s2_done, s2_evac, res_ready = map(
            sem, ("s1_done", "gelu_done", "h_ready", "s2_done", "s2_evac", "res_ready"))

        block = ctx.enter_context(nc.Block())

        def upto(n):
            return n + 1

        def start_counts(eng, *counters):
            for s in counters:
                eng.sem_inc(s, 1)

        def wait_apart(eng, s, value):
            eng.wait_ge(s, value)
            eng.sem_inc(passed, 1)

        def rows_rep(w):
            return w[KF * P:C, :]

        def load_split(eng, dst, w, s):
            eng.dma_start(dst[:, 0:KF, :], w[0:KF * P, :].rearrange("(k p) n -> p k n", p=P)).then_inc(s, 16)
            for r in range(REP):
                eng.dma_start(dst[CR * r:CR * (r + 1), KF, :], rows_rep(w)).then_inc(s, 16)

        SPLIT_LD = 16 * (REP + 1)

        def rep_last(ap, n):
            return ap[:, KF * P:C].unsqueeze(1).broadcast_to([ap.shape[0], n, CR])

        def order(more):
            new = (lambda *jobs: [("new", j) for j in jobs]) if more else (lambda *jobs: [])

            def own(*jobs):
                return [("own", j) for j in jobs]
            T1, QK, V, OT, PJ, T2, LG = ([(k, i) for i in range(n)] for k, n in (
                ("T1", 4), ("QK", 8), ("V", 4), ("OT", 4), ("PJ", 4), ("T2", 4), ("LG", 4)))
            return [
                ("scores", 0), ("max", 1), *own(V[1], V[2]), ("values", 0), ("move", 1), *own(V[3], OT[0]),
                ("scores", 1), ("max", 2), *own(PJ[0]), *new(T1[0], T1[1]), ("values", 1), ("move", 2),
                *new(T1[2], T1[3]), *own(OT[1]),
                ("scores", 2), ("max", 3), *own(PJ[1], T2[0]), ("values", 2), ("move", 3), *own(LG[0], OT[2], T2[1]),
                ("scores", 3), *new(QK[0]), *own(PJ[2], LG[1]), ("values", 3), *new(QK[1], QK[2]), *own(OT[3]),
                *new(QK[3], QK[4]), *own(PJ[3], T2[2]), *new(QK[5], QK[6]), *own(LG[2]), *new(QK[7], V[0]),
                *own(T2[3]), *([("max", 4)] if more else []), *own(LG[3]), *([("move", 4)] if more else []),
            ]

        def schedule(c, more):
            n = 0
            for what, arg in order(more):
                if what in ("own", "new"):
                    yield "job", arg, c + 1 if what == "new" else c, 2 + n % 2
                    n += 1
                else:
                    yield what, arg, c, None
            assert n % 2 == 0 or not more

        def first_jobs():
            jobs = [("T1", i) for i in range(4)] + [("QK", i) for i in range(8)] + [("V", 0)]
            return [(j, 0, 3 - n % 2) for n, j in enumerate(jobs)]

        @block.sync
        def _(sp):
            sp.dma_start(c_sb[:, 0, :], cond).then_inc(ld_c, 16)
            sp.dma_start(w_ada_sb[:, 0:KF, :],
                         w_ada[0:KF * P, :].rearrange("(k p) n -> p k n", p=P)).then_inc(ld_ada, 16)
            sp.dma_start(w_ada_sb[0:CR, KF, :], rows_rep(w_ada)).then_inc(ld_ada, 16)
            sp.dma_start(w_ada_sb[CR:CR + 1, KF, :], b_ada.unsqueeze(0)).then_inc(ld_ada, 16)
            for c in range(NC):
                sp.dma_start(x_sb[:, TPC * c:TPC * (c + 1), :],
                             x_v[:, TPC * c:TPC * (c + 1), :]).then_inc(ld_x, 16)
            sp.wait_ge(mod_ready, 1)
            sp.dma_start(mods_dram, mod_sb).then_inc(mods_out, 16)
            sp.wait_ge(mods_out, 16)

            def spread(dst, c, first, n, s):
                for q in range(SEQS):
                    sp.dma_start(dst[N * q:N * (q + 1)],
                                 mods_v[q, bass.ds(TPC * c, TPC), first:first + n * C].rearrange(
                                     "i (k c) -> i k c", c=C).partition_broadcast(N)).then_inc(s, 16)

            spread(mods1, 0, SH_A, 2, ld_mods1)
            with sp.Fori(0, NC - 1) as c:
                sp.wait_ge(x2_ready, upto(TPC * c))
                sp.wait_ge(y2_ready, upto(TPC * c))
                spread(mods2, c, G_A, 3, ld_mods2)
                sp.wait_ge(y1_ready, upto(c + 1))
                spread(mods1, c + 1, SH_A, 2, ld_mods1)
            sp.wait_ge(y2_ready, upto(NT - TPC))
            sp.wait_ge(x2_ready, upto(NT - TPC))
            spread(mods2, NC - 1, G_A, 3, ld_mods2)
            sp.wait_ge(mx_done, upto(NT))
            load_split(sp, w1_raw, w1[0], ld_w1)
            sp.wait_ge(pv_done, upto(NT))
            sp.dma_start(w2_raw[:], w2[0].rearrange("(p j) c -> p j c", j=HJ)).then_inc(ld_w2, 16)
            sp.wait_ge(xn_ready, upto(NT))
            sp.wait_ge(lg_ready, upto(NT))
            for e in range(E):
                sp.dma_start(b2_b[:, e, :], b2[e, :].partition_broadcast(P)).then_inc(ld_b2, 16)
            with sp.Fori(0, E - 1) as e:
                sp.wait_ge(w1_ready, e + 1)
                w1_next = w1[bass.ds(e + 1, 1), :, :].rearrange("a c h -> (a c) h")
                load_split(sp, w1_raw, w1_next, ld_w1)
                sp.wait_ge(w2_ready, e + 1)
                sp.dma_start(w2_raw[:, :, :],
                             w2[bass.ds(e + 1, 1), :, :].rearrange("a (p j) c -> (a p) j c", j=HJ)).then_inc(ld_w2, 16)
            for c in range(NC):
                if c >= 2:
                    sp.wait_ge(res_ready, c - 1)
                for q in range(SEQS):
                    sp.dma_start(gm[N * q:N * (q + 1), c % 2, :, :],
                                 mods_v[q, TPC * c:TPC * (c + 1), G_M:G_M + C].partition_broadcast(N)
                                 ).then_inc(ld_gm[c % 2], 16)
                if c >= 1:
                    sp.wait_ge(res_ready, c)
                    sp.dma_start(out_v[:, TPC * (c - 1):TPC * c, :],
                                 x_sb[:, TPC * (c - 1):TPC * c, :]).then_inc(stored, 16)
            sp.wait_ge(res_ready, NC)
            sp.dma_start(out_v[:, TPC * (NC - 1):NT, :], x_sb[:, TPC * (NC - 1):NT, :]).then_inc(stored, 16)
            sp.wait_ge(stored, 16 * NC)

        @block.gpsimd
        def _(pool):
            nc.gpsimd.memset(ident[:], 0.0).then_inc(pool_chain, 1)
            pool.wait_ge(pool_chain, 1)
            nc.gpsimd.affine_select(out=ident[:], in_=ident[:], compare_op=ALU.not_equal, fill=1.0, base=0,
                                    pattern=[[-1, P]], channel_multiplier=1).then_inc(ident_ready, 1)
            nc.gpsimd.memset(bqk[:, 0, :], 0.0).then_inc(bias_set, 1)
            nc.gpsimd.memset(bqk[:, 1, :], 1.0).then_inc(bias_set, 1)
            nc.gpsimd.memset(wqk[:, 0:3].bitcast(FP32), 0.0).then_inc(pads_ready, 1)
            nc.gpsimd.memset(wqk[:, 3:5].bitcast(FP32), 0.0).then_inc(pads_ready, 1)
            nc.gpsimd.memset(minus_half[:], -0.5).then_inc(pool_chain, 1)
            nc.gpsimd.memset(va[:], 1.0).then_inc(consts_ready, 1)
            nc.gpsimd.memset(mpad[:], 0.0).then_inc(consts_ready, 1)
            start_counts(pool, y1_ready, y2_ready, rstd2_ready)
            nc.gpsimd.memset(tri[:], 1.0).then_inc(pool_chain, 1)
            pool.wait_ge(pool_chain, 3)
            nc.gpsimd.affine_select(out=tri[:], in_=tri[:], compare_op=ALU.is_gt, fill=0.0, base=0,
                                    pattern=[[1, E], [-1, E]], channel_multiplier=0).then_inc(consts_ready, 1)
            pool.wait_ge(var1_ready, 1)
            nc.gpsimd.tensor_scalar(rstd[:], mv[:, :, 1], EPS, None, ALU.add).then_inc(pool_chain, 1)
            pool.wait_ge(pool_chain, 4)
            nc.gpsimd.tensor_tensor(rstd[:], rstd[:], minus_half[:], ALU.pow).then_inc(rstd1_ready, 1)

            def modulate1(c):
                pool.wait_ge(ld_mods1, 16 * SEQS * c + 16 * SEQS)
                pool.wait_ge(y1_norm, upto(TPC * c + TPC))
                nc.gpsimd.tensor_tensor(y1[:, :, 0:C], y1[:, :, 0:C], mods1[:, :, 1, :], ALU.mult).then_inc(pool_chain, 1)

            def modulate1_shift(c, links):
                pool.wait_ge(pool_chain, links)
                nc.gpsimd.tensor_tensor(y1[:, :, C:CX].rearrange("p i (r n) -> p i r n", n=CR),
                                        y1[:, :, KF * P:C].unsqueeze(2).broadcast_to([P, TPC, REP - 1, CR]),
                                        mods1[:, :, 0, KF * P:C].unsqueeze(2).broadcast_to([P, TPC, REP - 1, CR]),
                                        ALU.add).then_inc(pool_chain, 1)
                pool.wait_ge(pool_chain, links + 1)
                nc.gpsimd.tensor_tensor(y1[:, :, 0:C], y1[:, :, 0:C], mods1[:, :, 0, :], ALU.add).then_inc(y1_ready, 1)

            def tile_norm(t, c, links):
                wait_apart(pool, var2_ready, upto(TPC * c + t + 1))
                nc.gpsimd.tensor_scalar(rstd2[:, t % 2:t % 2 + 1], mv2[:, t % 2, 1:2], EPS, None,
                                        ALU.add).then_inc(pool_chain, 1)
                pool.wait_ge(pool_chain, links)
                nc.gpsimd.tensor_tensor(rstd2[:, t % 2:t % 2 + 1], rstd2[:, t % 2:t % 2 + 1], minus_half[:, 0:1],
                                        ALU.pow).then_inc(rstd2_ready, 1)
                pool.wait_ge(y2_norm, upto(TPC * c + t + 1))
                y = y2[:, t % 2, 0:C]
                nc.gpsimd.tensor_tensor(y, y, mods2[:, t, 2, :], ALU.mult).then_inc(pool_chain, 1)
                pool.wait_ge(pool_chain, links + 1)
                nc.gpsimd.tensor_tensor(y2[:, t % 2, C:CX].rearrange("p (r n) -> p r n", n=CR),
                                        rep_last(y, REP - 1), rep_last(mods2[:, t, 1, :], REP - 1),
                                        ALU.add).then_inc(pool_chain, 1)
                pool.wait_ge(pool_chain, links + 2)
                nc.gpsimd.tensor_tensor(y, y, mods2[:, t, 1, :], ALU.add).then_inc(y2_ready, 1)

            def chunk(c, more):
                links = 6 + LINKS * c
                pool.wait_ge(ld_mods2, 16 * SEQS * c + 16 * SEQS)
                if more:
                    modulate1(c + 1)
                    modulate1_shift(c + 1, links + 1)
                    links += 2
                for t in range(TPC):
                    tile_norm(t, c, links + 1)
                    links += 3

            LINKS = 2 + 3 * TPC
            modulate1(0)
            modulate1_shift(0, 5)
            for weight_split in (wqk_ready, wv_ready, wp_ready):
                pool.wait_ge(weight_split, 1)
            nc.gpsimd.memset(kblk[:], 0.0).then_inc(kblk_zero, 1)
            with pool.Fori(0, NC - 1) as c:
                chunk(c, True)
            chunk(NC - 1, False)
            pool.wait_ge(lg_ready, upto(NT))
            pool.wait_ge(xn_ready, upto(NT))
            nc.gpsimd.memset(acc[:], 0.0).then_inc(acc_zero, 1)

        @block.scalar
        def _(act):
            load_split(act, wqkv_raw, w_qkv, ld_qkv)
            act.dma_start(bv_b[:], b_qkv[2 * C:3 * C].partition_broadcast(P)).then_inc(ld_small, 16)
            act.dma_start(bp_b[:], b_proj.partition_broadcast(P)).then_inc(ld_small, 16)
            act.wait_ge(bias_set, 2)
            for qk in range(2):
                for i in range(4):
                    act.dma_start(bqk[HW * i:HW * i + HD, qk, :],
                                  b_qkv[qk * C:(qk + 1) * C].rearrange("(g i d) -> i d g", i=4, d=HD)[i],
                                  allow_slow_non_contiguous=True).then_inc(ld_bqk, 16)
            act.dma_start(wg[:, 0:KF, :], w_gate[0:KF * P, :].rearrange("(k p) n -> p k n", p=P)).then_inc(ld_small, 16)
            act.dma_start(wg[0:CR, KF, :], rows_rep(w_gate)).then_inc(ld_small, 16)
            load_split(act, wp_raw, w_proj, ld_wp)
            act.dma_start(b1_sb[:], b1.rearrange("e (p j) -> p e j", j=HJ)).then_inc(ld_b1, 16)
            act.wait_ge(ld_c, 16)
            nc.scalar.activation(c_sb[:, 1, :], c_sb[:, 0, :], ACT.Exp, scale=-1.0).then_inc(e_ready, 1)
            act.wait_ge(bqk_ready, 1)
            act.wait_ge(mod_ready, 1)
            act.wait_ge(mods_out, 16)

            def copy(dst, src):
                return nc.scalar.activation(dst, src, ACT.Copy)

            def hi_of_tile(dst, bank):
                return copy(dst, ps[:, bank, 0:KT * P].rearrange("p (k t) -> p k t", t=P))

            def job(name, c, bank):
                kind, i = name
                if kind == "T1":
                    act.wait_ge(t1_done, upto(TPC * c + i + 1))
                    hi_of_tile(h1[:, 0:KT, P * i:P * (i + 1)], bank).then_inc(h1_hi, 1)
                elif kind == "QK":
                    qk, g = (1, i) if i < HG else (0, i - HG)
                    if i == 0:
                        act.wait_ge(st_done, upto(TPC * c))
                    act.wait_ge(qk_done, upto(2 * HG * c + i + 1))
                    bias = bqk[:, qk, g:g + 1]
                    if qk:
                        act.wait_ge(kblk_ready, upto(HG * c))
                        nc.scalar.activation(kTb[:, g, :], ps[:, bank, :], ACT.Identity, bias=bias,
                                             scale=1.0).then_inc(kTb_ready, 1)
                        nc.scalar.activation(kT[:, g, :], ps[:, bank, :], ACT.Identity, bias=bias,
                                             scale=1.0).then_inc(qk_read, 1)
                    else:
                        nc.scalar.activation(qT[:, g, :], ps[:, bank, :], ACT.Identity, bias=bias, scale=SCALE)
                        nc.scalar.activation(qTb[:, g, :], ps[:, bank, :], ACT.Identity, bias=bias,
                                             scale=SCALE).then_inc(qk_read, 1)
                elif kind == "OT":
                    act.wait_ge(ot_done, upto(TPC * c + i + 1))
                    act.wait_ge(pj_done, upto(TPC * c + max(i - 1, 0)))
                    hi_of_tile(ox[:, i % 2, 0:KT], bank).then_inc(ox_hi, 1)
                elif kind == "T2":
                    act.wait_ge(t2_done, upto(TPC * c + i + 1))
                    act.wait_ge(lg_done, upto(TPC * c + max(i - 1, 0)))
                    act.wait_ge(xn_ready, upto(TPC * c + max(i - 1, 0)))
                    copy(yT[:, i % 2], ps[:, bank, 0:KT * P].rearrange("p (k t) -> p k t", t=P)
                         ).then_inc(yT_ready, 1)
                    wait_apart(act, yT_ready, upto(TPC * c + i + 1))
                    copy(xn_all[:, 0:KT, bass.ds(P * (TPC * c + i), P)], yT[:, i % 2]).then_inc(xn_hi, 1)

            def softmax(t, c):
                act.wait_ge(st_done, upto(TPC * c + t + 1))
                act.wait_ge(pv_done, upto(TPC * c + t))
                nc.scalar.activation(pT[:].rearrange("p i g q -> p i (g q)"), ps[:, 4:8, 0:HG * N],
                                     ACT.Exp).then_inc(exp_done, 1)

            start_counts(act, kTb_ready, h1_hi, qk_read, ox_hi, yT_ready, xn_hi, exp_done,
                         gelu_done)
            for name, c, bank in first_jobs():
                job(name, c, bank)

            def chunk(c, more):
                for what, name, k, bank in schedule(c, more):
                    if what == "scores":
                        softmax(name, c)
                    elif what == "job":
                        job(name, k, bank)

            with act.Fori(0, NC - 1) as c:
                chunk(c, True)
            chunk(NC - 1, False)
            act.wait_ge(rmax_ready, 1)
            nc.scalar.activation(r_exp[:], r_exp[:], ACT.Exp).then_inc(rexp_ready, 1)

            w1_in = w1_raw[:].rearrange("p k (q j) -> p k j q", j=HJ)

            def w1_hi(e):
                act.wait_ge(ld_w1, SPLIT_LD * e + SPLIT_LD)
                act.wait_ge(s1_done, upto(NC * HJ * e))
                for k in range(KT):
                    nc.scalar.activation(w1s[:, k], w1_in[:, k], ACT.Copy).then_inc(w1hi, 1)

            def w2_hi(e):
                act.wait_ge(ld_w2, 16 * e + 16)
                act.wait_ge(s2_done, upto(NT * e))
                nc.scalar.activation(w2s[:, 0], w2_raw[:], ACT.Copy).then_inc(w2hi, 1)

            def expert(e, last):
                w2_hi(e)
                for c in range(NC):
                    for j in range(HJ):
                        n = HJ * c + j
                        act.wait_ge(s1_done, upto(NC * HJ * e + n + 1))
                        wait_apart(act, h_ready, upto(NC * HJ * e + max(n - 1, 0)))

                        nc.scalar.activation(h32[:, n % 2, :], ps[:, n % 4, :], ACT.Gelu_apprx_tanh,
                                             bias=b1_sb[:, bass.ds(e, 1), j:j + 1].rearrange("p a b -> p (a b)"),
                                             ).then_inc(gelu_done, 1)
                if not last:
                    w1_hi(e + 1)

            act.wait_ge(ld_b1, 16)
            act.wait_ge(lg_ready, upto(NT))
            act.wait_ge(xn_ready, upto(NT))
            w1_hi(0)
            with act.Fori(0, E - 1) as e:
                expert(e, False)
            expert(E - 1, True)

        @block.vector
        def _(dve):
            V = nc.vector
            chain = [0, 0]

            def link(ins, base=0):
                chain[0] += 1
                ins.then_inc(dve_chain, 1)
                dve.wait_ge(dve_chain, base + chain[0])

            def split_weight(dst, raw, s):
                for k in range(KT):
                    last = V.tensor_copy(dst(k), raw(k))
                link(last)
                for k in range(KF):
                    V.tensor_tensor(dst(LO + k), raw(k), dst(k), ALU.subtract)
                for r in (1, 3):
                    rr = slice(CR * r, CR * (r + 1))
                    last = V.tensor_tensor(dst(REST)[rr], raw(KF)[rr], dst(REST)[rr], ALU.subtract)
                last.then_inc(s, 1)

            V.memset(sT[CR:CR + 1, KF, :], 1.0).then_inc(ident_ready, 1)
            dve.wait_ge(e_ready, 1)
            link(V.tensor_scalar(c_sb[:, 1, :], c_sb[:, 1, :], 1.0, None, ALU.add))
            link(V.reciprocal(c_sb[:, 2, :], c_sb[:, 1, :]))
            V.tensor_tensor(c_sb[:, 2, :], c_sb[:, 2, :], c_sb[:, 0, :], ALU.mult).then_inc(s_ready, 1)
            dve.wait_ge(ld_qkv, SPLIT_LD)
            dve.wait_ge(pads_ready, 2)
            qk_raw = wqkv_raw[:, :, 0:2 * C].rearrange("p k (h d) -> p k h d", d=HD)
            split_weight(lambda s: wqk[:, s, :, 0:HD], lambda k: qk_raw[:, k], wqk_ready)
            dve.wait_ge(sT_done, 1)
            V.tensor_copy(sT[:, 0:KF, :], ps[:, 0, 0:KF * B].rearrange("p (k b) -> p k b", b=B))
            V.tensor_copy(sT[0:CR, KF, :], ps[0:CR, 0, KF * B:KT * B]).then_inc(sT_ready, 1)
            split_weight(lambda s: wv[:, s, :], lambda k: wqkv_raw[:, k, 2 * C:3 * C], wv_ready)
            dve.wait_ge(mod_done, 1)
            link(V.tensor_copy(mod_sb.rearrange("b (g n) -> b g n", n=MODN), ps[0:B, 1:5, 0:MODN]))
            V.tensor_scalar(mod_sb[:, SC_A:SC_A + C], mod_sb[:, SC_A:SC_A + C], 1.0, None, ALU.add)
            V.tensor_scalar(mod_sb[:, SC_M:SC_M + C], mod_sb[:, SC_M:SC_M + C], 1.0, None,
                            ALU.add).then_inc(mod_ready, 1)
            dve.wait_ge(ld_x, 16 * NC)
            for t in range(NT):
                last = V.bn_stats(stats[:, t, :], x_sb[:, t, :])
            link(last)
            for t in range(NT):
                last = V.bn_aggr(mv[:, t, :], stats[:, t, :])
            last.then_inc(var1_ready, 1)
            dve.wait_ge(ld_bqk, 8 * 16)
            V.tensor_scalar(bqk[:, 0, :], bqk[:, 0, :], SCALE, None, ALU.mult).then_inc(bqk_ready, 1)
            dve.wait_ge(ld_wp, SPLIT_LD)
            split_weight(lambda s: wp[:, s, :], lambda k: wp_raw[:, k, :], wp_ready)
            dve.wait_ge(rstd1_ready, 1)
            dve.wait_ge(consts_ready, 3)
            dve.wait_ge(ld_small, 4 * 16)
            start_counts(dve, kblk_ready, y1_norm, h1_ready, v_ready, red_done, add_done, o_ready, ox_ready, pj_read, x2_ready,
                         var2_ready, y2_norm, xn_ready, lg_ready, h_ready, s2_evac)

            def x_tile(c, i):
                return x_sb[:, bass.ds(TPC * c + i, 1), :].rearrange("p a c -> p (a c)")

            def norm1(c):
                dve.wait_ge(t1_done, upto(TPC * c))
                for i in range(TPC):
                    V.tensor_scalar(y1[:, i, 0:C], x_tile(c, i),
                                    mv[:, bass.ds(TPC * c + i, 1), 0:1].rearrange("p a b -> p (a b)"),
                                    rstd[:, bass.ds(TPC * c + i, 1)], ALU.subtract, ALU.mult).then_inc(y1_norm, 1)

            def lo_of_tile(dst, src):
                V.tensor_tensor(dst[:, LO:LO + KF], src[:, 0:KF], dst[:, 0:KF], ALU.subtract)
                lo = slice(2 * CR, P)
                return V.tensor_tensor(dst[lo, REST], src[lo, KF], dst[lo, REST], ALU.subtract)

            def neg_max(t, c):
                dve.wait_ge(mx_done, upto(TPC * c + t + 1))
                dve.wait_ge(mt_done, upto(TPC * c + t))
                V.tensor_reduce(mpad[:].rearrange("p g (i w) -> p g i w", w=HW)[:, :, :, HD],
                                ps[:, 0:2, :].rearrange("p b (g i k) -> p (b g) i k", i=4, k=N),
                                AX.X, ALU.max, negate=True).then_inc(red_done, 1)

            def add_max(t, c):
                dve.wait_ge(mt_done, upto(TPC * c + t + 1))
                q = qT[:, :, P * (t % TPC):P * (t % TPC + 1)]
                V.tensor_tensor(q, q, ps[:, 0, :].rearrange("p (g q) -> p g q", q=P), ALU.add).then_inc(add_done, 1)

            def normalise(t, c, base):
                dve.wait_ge(pv_done, upto(TPC * c + t + 1))
                for q in range(SEQS):
                    rows = slice(N * q, N * (q + 1))
                    o_ps = ps[rows, 4 + q, 0:NH * VW].rearrange("p (h d) -> p h d", d=VW)
                    last = V.reciprocal(rden[rows, :], o_ps[:, :, HD])
                link(last, base)
                for q in range(SEQS):
                    rows = slice(N * q, N * (q + 1))
                    o_ps = ps[rows, 4 + q, 0:NH * VW].rearrange("p (h d) -> p h d", d=VW)
                    last = V.tensor_tensor(o_sb[rows, t % 2, 0:C].rearrange("p (h d) -> p h d", d=HD),
                                           o_ps[:, :, 0:HD], rden[rows, :].unsqueeze(2).broadcast_to([N, NH, HD]),
                                           ALU.mult)
                link(last, base)
                V.tensor_copy(o_sb[:, t % 2, C:CX].rearrange("p (r n) -> p r n", n=CR),
                              rep_last(o_sb[:, t % 2, :], REP - 1)).then_inc(o_ready, 1)

            def norm2(i, c):
                wait_apart(dve, rstd2_ready, upto(TPC * c + i + 1))
                dve.wait_ge(t2_done, upto(TPC * c + max(i - 1, 0)))
                V.tensor_scalar(y2[:, i % 2, 0:C], x_tile(c, i), mv2[:, i % 2, 0:1], rstd2[:, i % 2:i % 2 + 1],
                                ALU.subtract, ALU.mult).then_inc(y2_norm, 1)

            def job(name, c, bank, base):
                kind, i = name
                n = upto(TPC * c + i + 1)
                if kind == "T1":
                    dve.wait_ge(h1_hi, n)
                    lo_of_tile(h1[:, :, P * i:P * (i + 1)],
                               ps[:, bank, 0:KT * P].rearrange("p (k t) -> p k t", t=P)).then_inc(h1_ready, 1)
                elif kind == "QK":
                    if i == 0:
                        dve.wait_ge(mx_done, upto(TPC * c))
                    dve.wait_ge(kTb_ready, upto(HG * c + i + 1))
                    for h in range(4):
                        rows = slice(HW * h, HW * (h + 1))
                        last = V.tensor_copy(kblk[rows, i, :, h, :], kTb[rows, i].rearrange("p (b n) -> p b n", n=N))
                    last.then_inc(kblk_ready, 1)
                elif kind == "V":
                    dve.wait_ge(v_done, n)
                    V.tensor_tensor(va[:, i, :, 0:HD], ps[:, bank, 0:C].rearrange("p (h d) -> p h d", d=HD),
                                    bv_b[:].rearrange("p (h d) -> p h d", d=HD), ALU.add).then_inc(v_ready, 1)
                elif kind == "OT":
                    dve.wait_ge(ox_hi, n)
                    lo_of_tile(ox[:, i % 2], ps[:, bank, 0:KT * P].rearrange("p (k t) -> p k t", t=P)
                               ).then_inc(ox_ready, 1)
                elif kind == "PJ":
                    dve.wait_ge(pj_done, n)
                    V.tensor_tensor(pj[:, i % 2, :], ps[:, bank, 0:C], bp_b[:], ALU.add).then_inc(pj_read, 1)
                    dve.wait_ge(ld_mods2, 16 * SEQS * c + 16 * SEQS)
                    dve.wait_ge(pj_read, n)
                    link(V.tensor_tensor(pj[:, i % 2, :], pj[:, i % 2, :], mods2[:, i, 0, :], ALU.mult), base)
                    V.tensor_tensor(x_tile(c, i), x_tile(c, i), pj[:, i % 2, :], ALU.add).then_inc(x2_ready, 1)
                    wait_apart(dve, x2_ready, n)
                    link(V.bn_stats(stats2[:, i % 2, :], x_tile(c, i)), base)
                    dve.sem_inc(passed, 1)
                    V.bn_aggr(mv2[:, i % 2, :], stats2[:, i % 2, :]).then_inc(var2_ready, 1)
                elif kind == "T2":
                    dve.wait_ge(xn_hi, n)
                    lo_of_tile(xn_all[:, :, bass.ds(P * (TPC * c + i), P)], yT[:, i % 2]).then_inc(xn_ready, 1)
                elif kind == "LG":
                    dve.wait_ge(lg_done, n)
                    V.tensor_copy(logits[:, bass.ds(TPC * c + i, 1), :].rearrange("p a e -> p (a e)"),
                                  ps[:, bank, 0:E]).then_inc(lg_ready, 1)

            def chunk(c, more, base):
                if more:
                    norm1(c + 1)
                waiting = None
                for what, name, k, bank in schedule(c, more):
                    if what == "max":
                        neg_max(name, c)
                    elif what == "move":
                        add_max(name, c)
                    elif what == "values":
                        normalise(name, c, base)
                    elif what == "job" and not (name[0] == "QK" and name[1] >= HG):
                        job(name, k, bank, base)
                        if name[0] == "PJ":
                            waiting = name[1]
                            continue
                    else:
                        continue
                    if waiting is not None:
                        norm2(waiting, c)
                        waiting = None

            norm1(0)
            for name, c, bank in first_jobs():
                if name == ("QK", 0):
                    dve.wait_ge(kblk_zero, 1)
                if not (name[0] == "QK" and name[1] >= HG):
                    job(name, c, bank, 0)
            neg_max(0, 0)
            add_max(0, 0)
            LINKS = 4 * TPC
            before = chain[0]
            with dve.Fori(0, NC - 1) as c:
                chunk(c, True, LINKS * c)
                assert chain[0] - before == LINKS, chain[0] - before
            chain[0] = before + LINKS * (NC - 1)
            chunk(NC - 1, False, 0)
            dve.wait_ge(lg_ready, upto(NT))

            l_j = logits[:].unsqueeze(2).broadcast_to([P, NT, E, E])
            l_e = logits[:].unsqueeze(3).broadcast_to([P, NT, E, E])
            V.tensor_tensor(r_gt[:], l_j, l_e, ALU.is_gt)
            V.tensor_reduce(r_max[:], logits[:], AX.X, ALU.max)
            link(V.tensor_tensor(r_eq[:], l_j, l_e, ALU.is_equal))
            V.tensor_tensor(r_exp[:], logits[:], r_max[:].unsqueeze(2).broadcast_to([P, NT, E]),
                            ALU.subtract).then_inc(rmax_ready, 1)
            eq16 = r_eq[:].rearrange("p t e j -> p t (e j)")
            tri16 = tri[:].rearrange("p e j -> p (e j)").unsqueeze(1).broadcast_to([P, NT, E * E])
            link(V.tensor_tensor(eq16, eq16, tri16, ALU.mult))
            link(V.tensor_tensor(r_gt[:], r_gt[:], r_eq[:], ALU.add))
            link(V.tensor_reduce(r_sel[:], r_gt[:], AX.X, ALU.add))
            link(V.tensor_scalar(r_sel[:], r_sel[:], 1.5, None, ALU.is_lt))
            dve.wait_ge(rexp_ready, 1)
            link(V.tensor_tensor(r_sel[:], r_sel[:], r_exp[:], ALU.mult))
            link(V.tensor_reduce(r_sum[:], r_sel[:], AX.X, ALU.add))
            link(V.reciprocal(r_sum[:], r_sum[:]))
            V.tensor_tensor(cw[:].rearrange("p e t -> p t e"), r_sel[:],
                            r_sum[:].unsqueeze(2).broadcast_to([P, NT, E]), ALU.mult).then_inc(cw_ready, 1)
            dve.wait_ge(cw_ready, 1)

            w1_in = w1_raw[:].rearrange("p k (q j) -> p k j q", j=HJ)

            def w1_lo(e):
                dve.wait_ge(w1hi, KT * e + KT)
                for k in range(KF):
                    V.tensor_tensor(w1s[:, LO + k], w1_in[:, k], w1s[:, k], ALU.subtract)
                for r in (1, 3):
                    rr = slice(CR * r, CR * (r + 1))
                    last = V.tensor_tensor(w1s[rr, REST], w1_in[rr, KF], w1s[rr, REST], ALU.subtract)
                last.then_inc(w1_ready, 1)

            def w2_lo(e):
                dve.wait_ge(w2hi, e + 1)
                V.tensor_tensor(w2s[:, 1], w2_raw[:], w2s[:, 0], ALU.subtract).then_inc(w2_ready, 1)

            EL = NC * (HJ + TPC)

            def expert(e, last):
                before = chain[0]
                base = EL * e if not last else 0
                w2_lo(e)
                for c in range(NC):
                    dve.wait_ge(s2_done, upto(NT * e + TPC * c))
                    for j in range(HJ):
                        n = HJ * c + j
                        dve.wait_ge(gelu_done, upto(NC * HJ * e + n + 1))
                        link(V.tensor_copy(hs[:, 0, j, :], h32[:, n % 2, :]), base)
                        V.tensor_tensor(hs[:, 1, j, :], h32[:, n % 2, :], hs[:, 0, j, :],
                                        ALU.subtract).then_inc(h_ready, 1)
                    if c == NC - 1 and not last:
                        w1_lo(e + 1)
                    for i in range(TPC):
                        t = TPC * c + i
                        dve.wait_ge(s2_done, upto(NT * e + t + 1))
                        link(V.tensor_tensor(yt[:, i % 2, :], ps[:, 4 + i, 0:C],
                                             b2_b[:, bass.ds(e, 1), :].rearrange("p a c -> p (a c)"), ALU.add), base)
                        V.scalar_tensor_tensor(acc[:, t, :], yt[:, i % 2, :],
                                               cw[:, bass.ds(e, 1), t:t + 1].rearrange("p a b -> p (a b)"),
                                               acc[:, t, :], ALU.mult, ALU.add).then_inc(s2_evac, 1)
                    if last:
                        tiles = slice(TPC * c, TPC * (c + 1))
                        dve.wait_ge(ld_gm[c % 2], 16 * (P // N) * (c // 2 + 1))
                        dve.wait_ge(s2_evac, upto(NT * e + TPC * (c + 1)))
                        link(V.tensor_tensor(gm[:, c % 2], gm[:, c % 2], acc[:, tiles, :], ALU.mult), base)
                        V.tensor_tensor(x_sb[:, tiles, :], x_sb[:, tiles, :], gm[:, c % 2],
                                        ALU.add).then_inc(res_ready, 1)
                return chain[0] - before

            w1_lo(0)
            dve.wait_ge(ld_b2, 16 * E)
            dve.wait_ge(acc_zero, 1)
            with dve.Fori(0, E - 1) as e:
                n = expert(e, False)
                assert n == EL, n
            chain[0] += EL * (E - 2)
            expert(E - 1, True)

        @block.tensor
        def _(pe):
            M = nc.tensor.matmul

            def split_matmul(out_ap, stat, mov):
                for n, (a, b) in enumerate(PAIRS):
                    last = M(out_ap, stat(a), mov(b), start=(n == 0), stop=(n == len(PAIRS) - 1))
                return last

            pe.wait_ge(ident_ready, 2)
            pe.wait_ge(s_ready, 1)
            for k in range(KT):
                n = P if k < KF else CR
                last = nc.tensor.transpose(ps[0:n, 0, B * k:B * (k + 1)], c_sb[:, 2, P * k:P * k + n], ident[0:B, 0:B])
            last.then_inc(sT_done, 1)
            pe.wait_ge(sT_ready, 1)
            pe.wait_ge(ld_ada, 3 * 16)
            for g in range(4):
                cols = slice(MODN * g, MODN * (g + 1))
                o = ps[0:B, 1 + g, 0:MODN]
                for k in range(KT):
                    n = P if k < KF else CR + 1
                    last = M(o, sT[0:n, k, :], w_ada_sb[0:n, k, cols], start=(k == 0), stop=(k == KF))
            last.then_inc(mod_done, 1)
            pe.wait_ge(wqk_ready, 1)
            pe.wait_ge(wv_ready, 1)
            pe.wait_ge(wp_ready, 1)
            pe.wait_ge(ld_small, 4 * 16)

            def transpose_tile(rows, bank):
                for k in range(KT):
                    last = nc.tensor.transpose(ps[:, bank, P * k:P * (k + 1)], rows[:, P * k:P * (k + 1)], ident[:])
                return last

            def wait_read(name, c):
                kind, i = name
                reader, per_chunk = {"T1": (h1_ready, TPC), "QK": (qk_read, 2 * HG), "V": (v_ready, TPC),
                                     "OT": (ox_ready, TPC), "PJ": (pj_read, TPC), "T2": (yT_ready, TPC),
                                     "LG": (lg_ready, TPC)}[kind]
                pe.wait_ge(reader, upto(per_chunk * c + i + 1))

            def job(name, c, bank):
                kind, i = name
                n = upto(TPC * c + i + 1)
                if kind == "T1":
                    pe.wait_ge(y1_ready, upto(c + 1))
                    transpose_tile(y1[:, i, :], bank).then_inc(t1_done, 1)
                elif kind == "QK":
                    if i == 0:
                        pe.wait_ge(h1_ready, upto(TPC * c + TPC))
                    g, first_head = i % HG, (NH if i < HG else 0)
                    heads = slice(first_head + 4 * g, first_head + 4 * (g + 1))
                    split_matmul(ps[:, bank, :], lambda a: wqk[:, a, heads, :].rearrange("p h w -> p (h w)"),
                                 lambda b: h1[:, b, :]).then_inc(qk_done, 1)
                elif kind == "V":
                    split_matmul(ps[:, bank, 0:C], lambda a: h1[:, a, P * i:P * (i + 1)],
                                 lambda b: wv[:, b, :]).then_inc(v_done, 1)
                elif kind == "OT":
                    pe.wait_ge(o_ready, n)
                    transpose_tile(o_sb[:, i % 2, :], bank).then_inc(ot_done, 1)
                elif kind == "PJ":
                    pe.wait_ge(ox_ready, n)
                    split_matmul(ps[:, bank, 0:C], lambda a: ox[:, i % 2, a, :],
                                 lambda b: wp[:, b, :]).then_inc(pj_done, 1)
                elif kind == "T2":
                    pe.wait_ge(y2_ready, n)
                    transpose_tile(y2[:, i % 2, :], bank).then_inc(t2_done, 1)
                elif kind == "LG":
                    pe.wait_ge(yT_ready, n)
                    for k in range(KT):
                        rows = slice(0, P if k < KF else CR)
                        last = M(ps[:, bank, 0:E], yT[rows, i % 2, k, :], wg[rows, k, :],
                                 start=(k == 0), stop=(k == KF))
                    last.then_inc(lg_done, 1)

            def max_scores(t, c):
                if t % TPC == 0:
                    pe.wait_ge(kblk_ready, upto(4 * (c + t // TPC) + 4))
                    pe.wait_ge(qk_read, upto(2 * HG * (c + t // TPC) + 2 * HG))
                pe.wait_ge(add_done, upto(TPC * c + t))
                for g in range(HG):
                    for q in range(SEQS):
                        first = P * (t % TPC) + N * q
                        last = M(ps[N * q:N * (q + 1), g // 2, 4 * N * (g % 2):4 * N * (g % 2 + 1)],
                                 qTb[:, g, first:first + N],
                                 kblk[:, g, SEQS * (t % TPC) + q].rearrange("p i n -> p (i n)"), start=True, stop=True)
                last.then_inc(mx_done, 1)

            def move_max(t, c):
                pe.wait_ge(red_done, upto(TPC * c + t + 1))
                for g in range(HG):
                    last = nc.tensor.transpose(ps[:, 0, P * g:P * (g + 1)], mpad[:, g, :], ident[:])
                last.then_inc(mt_done, 1)

            def scores(t, c):
                pe.wait_ge(add_done, upto(TPC * c + t + 1))
                pe.wait_ge(o_ready, upto(TPC * c + t))
                for q in range(SEQS):
                    toks = slice(P * t + N * q, P * t + N * (q + 1))
                    for g in range(HG):
                        for i in range(4):
                            rows = slice(HW * i, HW * (i + 1))
                            last = M(ps[N * q:N * (q + 1), 4 + i, N * g:N * (g + 1)], kT[rows, g, toks],
                                     qT[rows, g, toks], start=True, stop=True)
                last.then_inc(st_done, 1)

            def weigh_values(t, c):
                pe.wait_ge(v_ready, upto(TPC * c + t + 1))
                wait_apart(pe, exp_done, upto(TPC * c + t + 1))
                for h in range(NH):
                    for q in range(SEQS):
                        rows = slice(N * q, N * (q + 1))
                        last = M(ps[rows, 4 + q, VW * h:VW * (h + 1)], pT[rows, h % 4, h // 4, :],
                                 va[rows, t, h, :], start=True, stop=True)
                last.then_inc(pv_done, 1)

            def chunk(c, more):
                pe.wait_ge(qk_read, upto(2 * HG * c + 2 * HG))
                pe.wait_ge(v_ready, upto(TPC * c + 1))
                pe.wait_ge(yT_ready, upto(TPC * c))
                pe.wait_ge(lg_ready, upto(TPC * c))
                jobs = []
                for what, name, k, bank in schedule(c, more):
                    if what == "scores":
                        scores(name, c)
                    elif what == "max":
                        max_scores(name, c)
                    elif what == "values":
                        weigh_values(name, c)
                    elif what == "move":
                        move_max(name, c)
                    else:
                        jobs.append((name, k))
                        if len(jobs) > 2:
                            wait_read(*jobs[-3])
                        job(name, k, bank)

            start_counts(pe, t1_done, qk_done, v_done, mx_done, mt_done, st_done, pv_done, ot_done, pj_done,
                         t2_done, lg_done, s1_done, s2_done)
            done = []
            for name, c, bank in first_jobs():
                done.append((name, c))
                if len(done) > 2:
                    wait_read(*done[-3])
                job(name, c, bank)
            max_scores(0, 0)
            move_max(0, 0)
            with pe.Fori(0, NC - 1) as c:
                chunk(c, True)
            chunk(NC - 1, False)

            def expert(e):
                for c in range(NC):
                    if c == 0:
                        pe.wait_ge(w1_ready, e + 1)
                        pe.wait_ge(gelu_done, upto(NC * HJ * e))
                    for j in range(HJ):
                        n = HJ * c + j
                        if n >= 4:
                            pe.wait_ge(gelu_done, upto(NC * HJ * e + n - 3))
                        split_matmul(ps[:, n % 4, :], lambda a: w1s[:, a, j, :],
                                     lambda b: xn_all[:, b, CT * c:CT * (c + 1)]).then_inc(s1_done, 1)
                    if c == 0:
                        pe.wait_ge(w2_ready, e + 1)
                    pe.wait_ge(s2_evac, upto(NT * e + TPC * c))
                    for i in range(TPC):
                        toks = slice(P * i, P * (i + 1))
                        for j in range(HJ):
                            if i == 0:
                                pe.wait_ge(h_ready, upto(NC * HJ * e + HJ * c + j + 1))
                            for n, (a, b) in enumerate(((0, 0), (0, 1), (1, 0))):
                                last = M(ps[:, 4 + i, 0:C], hs[:, a, j, toks], w2s[:, b, j, :],
                                         start=(j == 0 and n == 0), stop=(j == HJ - 1 and n == 2))
                        last.then_inc(s2_done, 1)

            pe.wait_ge(xn_ready, upto(NT))
            pe.wait_ge(lg_ready, upto(NT))
            with pe.Fori(0, E - 1) as e:
                expert(e)
            expert(E - 1)


_INS = ["x", "cond_1152", "L0_cond_w_adaln", "L0_cond_b_adaln", "L0_cond_w_qkv", "L0_cond_b_qkv", "L0_cond_w_proj",
        "L0_cond_b_proj", "L0_cond_w_gate", "L0_cond_w1", "L0_cond_b1", "L0_cond_w2", "L0_cond_b2"]


def kernel(**inputs):
    import numpy as _np
    import concourse.bacc as _bacc
    from concourse import mybir as _mybir
    from concourse.bass_utils import run_bass_kernel_spmd as _run

    nc = _bacc.Bacc("TRN2", target_bir_lowering=False, num_devices=1)
    arrays, args = {}, []
    for name in _INS:
        a = _np.ascontiguousarray(inputs[name])
        arrays[f"in_{name}_dram"] = a
        args.append(nc.dram_tensor(f"in_{name}_dram", a.shape, _mybir.dt.from_np(a.dtype), kind="ExternalInput").ap())
    out = nc.dram_tensor("out_dram", inputs["x"].shape, _mybir.dt.float32, kind="ExternalOutput").ap()
    adaln_moe_kernel(nc, *args, out)
    r = _run(nc, [arrays], core_ids=[0])
    return r.results[0]["out_dram"]
```

```python
from contextlib import ExitStack

import concourse.bass as bass
from concourse import mybir

FP32 = mybir.dt.float32
FP32R = mybir.dt.float32r
I32 = mybir.dt.int32
BF16 = mybir.dt.bfloat16
ALU = mybir.AluOpType
ACT = mybir.ActivationFunctionType
AX = mybir.AxisListType

P = 128
PAIRS = [(0, 0), (0, 3), (3, 0), (1, 1), (1, 4), (4, 1), (2, 2)]
REST, LO = 2, 3


def adaln_moe_kernel(nc, x, cond, w_ada, b_ada, w_qkv, b_qkv, w_proj, b_proj, w_gate, w1, b1, w2, b2, out):
    B, N, C = x.shape
    E, _, H = w1.shape
    NH = 16
    HD = C // NH
    T = B * N
    NT = T // P
    TPC = 4
    NC = NT // TPC
    CT = TPC * P
    BPC = CT // N
    KF = C // P
    CR = C - KF * P
    KT = KF + 1
    REP = P // CR
    CX = KT * P
    HG = NH // 4
    HW = 32
    VW = HD + 1
    HJ = H // P
    SCALE = float(HD) ** -0.5
    EPS = 1e-6
    MODN = 6 * C // 4
    IT = 2
    IR = IT * P
    ITEMS = T // IR
    TOP = 2
    MOST = TOP * ITEMS + E - 1
    ALL_ITEMS = MOST + ITEMS + 1
    REGION = T + 2 * IR
    XW = CX + 2 * E
    FT = 2
    POOL_J = 1
    SLOTS = 4
    FAR = 2.0 ** 15
    assert E * REGION < FAR
    SH_A, SC_A, G_A, SH_M, SC_M, G_M = (k * C for k in range(6))

    x_v = x.rearrange("b n c -> (b n) c").rearrange("(i p) c -> p i c", p=P)
    out_v = out.rearrange("b n c -> (b n) c").rearrange("(i p) c -> p i c", p=P)
    SEQS = P // N
    mods_dram = nc.dram_tensor("mods_scratch", [B, 6 * C], FP32, kind="Internal").ap()
    rows_dram = nc.dram_tensor("rows_scratch", [E * REGION, XW], FP32, kind="Internal").ap()
    res_dram = nc.dram_tensor("results_scratch", [TOP * T + IR, C], FP32, kind="Internal").ap()
    res_v = res_dram[0:TOP * T, :].rearrange("(s i p) c -> p s i c", p=P, s=TOP)
    mods_v = mods_dram.rearrange("(i s) c -> s i c", s=SEQS)

    ctx = ExitStack()
    with ctx:
        def sb(name, shape, dt=FP32, scope=ctx):
            return scope.enter_context(nc.sbuf_tensor(name, shape, dt))

        def sem(name):
            return ctx.enter_context(nc.semaphore(name))

        ps = ctx.enter_context(nc.psum_tensor("ps", [P, 8, 512], FP32))

        x_sb = sb("x_sb", [P, NT, C])
        s_att = ExitStack()
        kblk = sb("kblk", [P, HG, BPC, 4, N], BF16, s_att)
        pT = sb("pT", [P, 4, HG, N], FP32, s_att)
        s_att.close()
        s_low = ExitStack()
        res_low = sb("res_low", [P, NT, C], FP32, s_low)
        s_low.close()
        w1_raw = sb("w1_raw", [P, KT, H])
        w2_raw = sb("w2_raw", [P, HJ, C])
        stage_flat = w1_raw[:].rearrange("p k h -> p (k h)")
        assert 4 * C <= H
        wqkv_raw = stage_flat[:, 0:3 * C * KT].rearrange("p (k n) -> p k n", k=KT)
        wp_raw = stage_flat[:, 3 * C * KT:4 * C * KT].rearrange("p (k n) -> p k n", k=KT)
        s0 = ExitStack()
        w_ada_sb = sb("w_ada_sb", [P, KT, 6 * C], FP32, s0)
        s0.close()
        w1s = [sb("w1s_0", [P, 5, HJ, P], FP32R)]
        s_qk = ExitStack()
        qT = sb("qT", [P, HG, CT], FP32, s_qk)
        kT = sb("kT", [P, HG, CT], FP32, s_qk)
        qTb = sb("qTb", [P, HG, CT], BF16, s_qk)
        s_qk.close()
        w2s = [sb("w2s_0", [P, 2, HJ, C], FP32R)]
        ident = sb("ident", [P, P])
        b1_sb = sb("b1_sb", [P, E, HJ])
        b2_b = sb("b2_b", [P, E, C])
        minus_half = sb("minus_half", [P, NT])
        tri = sb("tri", [P, E, E])
        before = sb("before", [P, P])
        ones = sb("ones", [P, P])
        pad_rows = sb("pad_rows", [P, IT, XW])
        logits = sb("logits", [P, TPC, E])
        r_gt = sb("r_gt", [P, 2, E, E])
        r_eq = sb("r_eq", [P, 2, E, E])
        r_sel = sb("r_sel", [P, 2, E])
        r_exp = sb("r_exp", [P, 2, E])
        r_max = sb("r_max", [P, 2])
        r_sum = sb("r_sum", [P, 2])
        r_pos = sb("r_pos", [P, 2, E])
        r_masked = sb("r_masked", [P, 2, 2, E])
        r_ends = sb("r_ends", [P, 2, 2])
        places = sb("places", [P, 2, TPC, 2], I32)
        token = sb("token", [P, NT])
        token_i = sb("token_i", [P, NT], I32)
        first_i = sb("first_i", [P, E, ITEMS], I32)
        number_i = sb("number_i", [P, ALL_ITEMS], I32)
        count = sb("count", [P, E])
        i_first = sb("i_first", [P, E, ITEMS])
        i_in = sb("i_in", [P, E, ITEMS])
        i_n = sb("i_n", [P, E])
        i_tri = sb("i_tri", [P, E, E])
        i_before = sb("i_before", [P, E])
        i_skip = sb("i_skip", [P, E])
        i_number = sb("i_number", [P, ALL_ITEMS])
        i_from = sb("i_from", [P, ALL_ITEMS, E - 1])
        i_row = sb("i_row", [P, ALL_ITEMS])
        per_expert = sb("per_expert", [P, 3, E], I32)
        item_row = sb("item_row", [P, ALL_ITEMS], I32)
        early = sb("early", [P, 1], I32)

        sa = ExitStack()
        y2 = sb("y2", [P, TPC, XW], FP32, sa)
        mods1 = sb("mods1", [P, TPC, 2, C], FP32, sa)
        y1 = sb("y1", [P, TPC, CX], FP32, sa)
        wqk = sb("wqk", [P, 5, 2 * NH, HW], FP32R, sa)
        wv = sb("wv", [P, 5, C], FP32R, sa)
        wp = sb("wp", [P, 5, C], FP32R, sa)
        wg = sb("wg", [P, KT, E], FP32, sa)
        bqk = sb("bqk", [P, 2, HG], FP32, sa)
        bv_b = sb("bv_b", [P, C], FP32, sa)
        bp_b = sb("bp_b", [P, C], FP32, sa)
        stats = sb("stats", [P, NT, 6], FP32, sa)
        mv = sb("mv", [P, NT, 2], FP32, sa)
        rstd = sb("rstd", [P, NT], FP32, sa)
        mv2 = sb("mv2", [P, 2, 2], FP32, sa)
        stats2 = sb("stats2", [P, 2, 6], FP32, sa)
        rstd2 = sb("rstd2", [P, 2], FP32, sa)
        mods2 = sb("mods2", [P, TPC, 3, C], FP32, sa)
        yT = sb("yT", [P, 2, KT, P], FP32, sa)
        h1 = sb("h1", [P, 5, CT], FP32R, sa)
        va = sb("va", [P, TPC, NH, SEQS, VW], FP32, sa)
        mpad = sb("mpad", [P, HG, P], FP32, sa)
        rden = sb("rden", [N, 2, NH // 2, SEQS], FP32, sa)
        o_sb = sb("o_sb", [P, 2, CX], FP32, sa)
        ox = sb("ox", [P, 2, 5, P], FP32R, sa)
        pj = sb("pj", [P, 2, C], FP32, sa)
        assert 9 * C + KT * B <= TPC * 3 * C
        mods2_flat = mods2[:].rearrange("p i k c -> p (i k c)")
        mod_sb = mods2_flat[0:B, 0:6 * C]
        c_sb = mods2_flat[0:B, 6 * C:9 * C].rearrange("b (k c) -> b k c", c=C)
        sT = mods2_flat[:, 9 * C:9 * C + KT * B].rearrange("p (k b) -> p k b", b=B)
        kTb = sb("kTb", [P, HG, CT], BF16, sa)
        sa.close()
        res = sb("res", [P, SLOTS, FT, C])
        xr = sb("xr", [P, IT, XW])
        xT = sb("xT", [P, 5, IR], FP32R)
        next_w = sb("next_w", [P, IT, 2 * E])
        assert XW <= SLOTS * FT * C // TPC and SLOTS * FT * C + IT * XW + 5 * IR + 2 * IT * E <= \
            TPC * (XW + 2 * C + CX)
        w1s.append(sb("w1s_1", [P, 5, HJ, P], FP32R))
        w2s.append(sb("w2s_1", [P, 2, HJ, C], FP32R))
        h32 = sb("h32", [P, 2, IR])
        hs = sb("hs", [P, 2, HJ, IR], FP32R)
        item_w = sb("item_w", [P, IT])
        item_to = sb("item_to", [P, IT], I32)
        y_add = sb("y_add", [P, IT, C])
        y_out = sb("y_out", [P, IT, C])
        gm = sb("gm", [P, NT, C])

        ld_c, ld_ada, ld_x, ld_qkv, ld_wp = map(sem, ("ld_c", "ld_ada", "ld_x", "ld_qkv", "ld_wp"))
        ld_bqk, ld_small, ld_b1, ld_w1, ld_w2 = map(sem, ("ld_bqk", "ld_small", "ld_b1", "ld_w1", "ld_w2"))
        ld_mods1, ld_mods2, ld_b2, mods_out, stored = map(
            sem, ("ld_mods1", "ld_mods2", "ld_b2", "mods_out", "stored"))
        ld_rows, pads_out, scattered = sem("ld_rows"), sem("pads_out"), sem("scattered")
        rows_out, rows_sent, results_sent = sem("rows_out"), sem("rows_sent"), sem("results_sent")
        ld_res = [sem(f"ld_res{k}") for k in range(SLOTS)]
        ld_low, low_gated, low_added = sem("ld_low"), sem("low_gated"), sem("low_added")
        ld_gm, ld_x0 = sem("ld_gm"), sem("ld_x0")
        router_chain, early_ready = sem("router_chain"), sem("early_ready")
        pool_chain, ident_ready, bias_set, consts_ready, pads_ready = map(
            sem, ("pool_chain", "ident_ready", "bias_set", "consts_ready", "pads_ready"))
        wqk_ready, wv_ready, wp_ready, bqk_ready = map(sem, ("wqk_ready", "wv_ready", "wp_ready", "bqk_ready"))
        e_ready, s_ready, sT_done, sT_ready, mod_done, mod_ready = map(
            sem, ("e_ready", "s_ready", "sT_done", "sT_ready", "mod_done", "mod_ready"))
        var1_ready, rstd1_ready = sem("var1_ready"), sem("rstd1_ready")
        dve_chain, passed = sem("dve_chain"), sem("passed")
        y1_norm, y1_ready, y1_other, t1_done, h1_hi, h1_ready = map(sem, ("y1_norm", "y1_ready", "y1_other", "t1_done", "h1_hi", "h1_ready"))
        qk_done, qk_read, kTb_ready, qTb_ready, kblk_zero, kblk_ready, v_done, v_ready = map(sem, ("qk_done", "qk_read", "kTb_ready", "qTb_ready", "kblk_zero", "kblk_ready", "v_done", "v_ready"))
        mx_done, red_done, mt_done, add_done, st_done = map(
            sem, ("mx_done", "red_done", "mt_done", "add_done", "st_done"))
        exp_done, pv_done, o_ready = map(sem, ("exp_done", "pv_done", "o_ready"))
        ot_done, ox_hi, ox_ready, pj_done, pj_read, x2_ready = map(
            sem, ("ot_done", "ox_hi", "ox_ready", "pj_done", "pj_read", "x2_ready"))
        var2_ready, rstd2_ready, y2_norm, y2_ready, t2_done, yT_ready = map(
            sem, ("var2_ready", "rstd2_ready", "y2_norm", "y2_ready", "t2_done", "yT_ready"))
        lg_done, lg_ready, rmax_ready, rexp_ready, sel_ready, rt_done, rt_read, route_ready, items_ready = map(
            sem, ("lg_done", "lg_ready", "rmax_ready", "rexp_ready", "sel_ready", "rt_done", "rt_read",
                  "route_ready", "items_ready"))
        w1hi, w1_ready, w1_rest, w2hi, w2_ready, t_done, xT_hi, xT_ready, next_kept = map(
            sem, ("w1hi", "w1_ready", "w1_rest", "w2hi", "w2_ready", "t_done", "xT_hi", "xT_ready", "next_kept"))
        h_hi, w_kept = sem("h_hi"), sem("w_kept")
        s1_done, gelu_done, h_ready, s2_done, y_read, y_ready, res_ready = map(
            sem, ("s1_done", "gelu_done", "h_ready", "s2_done", "y_read", "y_ready", "res_ready"))

        block = ctx.enter_context(nc.Block())

        def upto(n):
            return n + 1

        def start_counts(eng, *counters):
            for s in counters:
                eng.sem_inc(s, 1)

        def wait_apart(eng, s, value):
            eng.wait_ge(s, value)
            eng.sem_inc(passed, 1)

        def rows_rep(w):
            return w[KF * P:C, :]

        def load_split(eng, dst, w, s):
            eng.dma_start(dst[:, 0:KF, :], w[0:KF * P, :].rearrange("(k p) n -> p k n", p=P)).then_inc(s, 16)
            for r in range(REP):
                eng.dma_start(dst[CR * r:CR * (r + 1), KF, :], rows_rep(w)).then_inc(s, 16)

        SPLIT_LD = 16 * (REP + 1)

        def rep_last(ap, n):
            return ap[:, KF * P:C].unsqueeze(1).broadcast_to([ap.shape[0], n, CR])

        def order(more):
            new = (lambda *jobs: [("new", j) for j in jobs]) if more else (lambda *jobs: [])

            def first(part):
                return [] if more else [("weights", part)]

            def own(*jobs):
                return [("own", j) for j in jobs]
            T1, QK, V, OT, PJ, T2, LG, RT = ([(k, i) for i in range(n)] for k, n in (
                ("T1", 4), ("QK", 8), ("V", 4), ("OT", 4), ("PJ", 4), ("T2", 4), ("LG", 4), ("RT", 2)))
            return [
                ("scores", 0), ("max", 1), *own(V[1]), ("values 0", 0), *own(V[2]), ("values 1", 0), ("move", 1),
                *own(V[3], OT[0]),
                ("scores", 1), ("max", 2), *own(PJ[0]), ("values 0", 1), *new(T1[0]), ("values 1", 1),
                ("move", 2), ("residual", 0), *own(OT[1]), *new(T1[1]), ("norm", 0),
                ("scores", 2), ("max", 3), *own(PJ[1], T2[0]), ("values 0", 2), *new(T1[2]), ("values 1", 2),
                ("move", 3), *own(LG[0]), ("residual", 1), *own(OT[2]), ("norm", 1), *new(T1[3]),
                ("scores", 3), *new(QK[0]), *own(T2[1], PJ[2]), ("values 0", 3), *own(LG[1]), ("values 1", 3),
                *new(QK[1]), *own(OT[3]), ("residual", 2), *first("w1 hi"), *new(QK[2]), *own(PJ[3]), ("norm", 2),
                ("residual", 3), *new(QK[3]), ("norm", 3), ("select", 0), *first("w1 lo"), *new(QK[4]), *own(T2[2]),
                *new(QK[5]), *own(RT[0]), *first("w2 hi"), *own(LG[2]), *first("w1 rest"), *new(QK[6]), *own(T2[3]),
                *new(QK[7]), *own(LG[3]), *([("max", 4)] if more else []), *new(V[0]),
                *([("move", 4)] if more else []), ("select", 1), *first("w2 lo"), *own(RT[1]),
            ]

        def schedule(c, more):
            n = 0
            for what, arg in order(more):
                if what in ("own", "new"):
                    yield "job", arg, c + 1 if what == "new" else c, 2 + n % 2
                    n += 1
                else:
                    yield what, arg, c, None
            assert n % 2 == 0 or not more

        def first_jobs():
            jobs = [("T1", i) for i in range(4)] + [("QK", i) for i in range(8)] + [("V", 0)]
            return [(j, 0, 3 - n % 2) for n, j in enumerate(jobs)]

        ROWS_OUT = 16 * TOP * TPC

        def unit_slot(j):
            half = j % 2
            return ps[:, j // 2 % 4, IR * half:IR * (half + 1)]

        def over_items(eng, e, item, *between):
            eng.wait_ge(items_ready, 1)
            items = eng.value_load(per_expert[0:1, 0, bass.ds(e, 1)], min_val=0, max_val=ITEMS)
            first = eng.value_load(per_expert[0:1, 1, bass.ds(e, 1)], min_val=0, max_val=MOST)
            for k, work in enumerate(between):
                with eng.If(items > k):
                    item(first + k)
                work(first)
            with eng.Fori(len(between), ITEMS) as k:
                with eng.If(k < items):
                    item(first + k)

        @block.sync
        def _(sp):
            sp.dma_start(c_sb[:, 0, :], cond).then_inc(ld_c, 16)
            sp.dma_start(x_sb[:, 0:TPC, :], x_v[:, 0:TPC, :]).then_inc(ld_x0, 16)
            sp.dma_start(w_ada_sb[:, 0:KF, :],
                         w_ada[0:KF * P, :].rearrange("(k p) n -> p k n", p=P)).then_inc(ld_ada, 16)
            sp.dma_start(w_ada_sb[0:CR, KF, :], rows_rep(w_ada)).then_inc(ld_ada, 16)
            sp.dma_start(w_ada_sb[CR:CR + 1, KF, :], b_ada.unsqueeze(0)).then_inc(ld_ada, 16)
            for c in range(1, NC):
                sp.dma_start(x_sb[:, TPC * c:TPC * (c + 1), :],
                             x_v[:, TPC * c:TPC * (c + 1), :]).then_inc(ld_x, 16)

            def send_modulation(half):
                sp.wait_ge(mod_ready, half + 1)
                cols = slice(2 * MODN * half, 2 * MODN * (half + 1))
                sp.dma_start(mods_dram[:, cols], mod_sb[:, cols]).then_inc(mods_out, 16)
                sp.wait_ge(mods_out, 16 * (half + 1))

            def spread(dst, c, first, n, s):
                for q in range(SEQS):
                    sp.dma_start(dst[N * q:N * (q + 1)],
                                 mods_v[q, bass.ds(TPC * c, TPC), first:first + n * C].rearrange(
                                     "i (k c) -> i k c", c=C).partition_broadcast(N)).then_inc(s, 16)

            send_modulation(0)
            spread(mods1, 0, SH_A, 2, ld_mods1)
            send_modulation(1)
            with sp.Fori(0, NC - 1) as c:
                sp.wait_ge(x2_ready, upto(TPC * c))
                sp.wait_ge(y2_ready, upto(TPC * c))
                spread(mods2, c, G_A, 3, ld_mods2)
                sp.wait_ge(y1_ready, upto(TPC * c + TPC))
                spread(mods1, c + 1, SH_A, 2, ld_mods1)
            sp.wait_ge(y2_ready, upto(NT - TPC))
            sp.wait_ge(x2_ready, upto(NT - TPC))
            spread(mods2, NC - 1, G_A, 3, ld_mods2)
            sp.wait_ge(early_ready, 1)
            n_early = sp.value_load(early[0:1, 0:1], min_val=0, max_val=T)
            sp.wait_ge(rows_sent, upto(NC - 1))
            sp.wait_ge(t1_done, upto(NT))
            with sp.If(n_early >= IR):
                sp.dma_start(xr[:], rows_dram[0:IR, :].rearrange("(i p) c -> p i c", p=P)).then_inc(ld_rows, 16)
            sp.wait_ge(mx_done, upto(NT))
            load_split(sp, w1_raw, w1[0], ld_w1)
            sp.wait_ge(pv_done, upto(NT))
            sp.dma_start(w2_raw[:], w2[0].rearrange("(p j) c -> p j c", j=HJ)).then_inc(ld_w2, 16)
            def load_next(e):
                sp.wait_ge(w1_ready, upto(e + 1))
                sp.wait_ge(w1_rest, upto(2 * e + 2))
                load_split(sp, w1_raw, w1[bass.ds(e + 1, 1), :, :].rearrange("a c h -> (a c) h"), ld_w1)
                sp.wait_ge(w2_ready, upto(2 * e + 2))
                sp.dma_start(w2_raw[:, :, :],
                             w2[bass.ds(e + 1, 1), :, :].rearrange("a (p j) c -> (a p) j c", j=HJ)).then_inc(ld_w2, 16)

            load_next(0)
            sp.wait_ge(items_ready, 1)
            end = [sp.value_load(per_expert[0:1, 2, e:e + 1], min_val=REGION * e, max_val=REGION * e + T)
                   for e in range(E)]

            def load_rows(n):
                row = sp.value_load(item_row[0:1, bass.ds(n, 1)], min_val=0, max_val=E * REGION - IR)
                sp.dma_start(xr[:], rows_dram[bass.ds(row, IR), :].rearrange("(i p) c -> p i c", p=P)
                             ).then_inc(ld_rows, 16)

            sp.wait_ge(rows_sent, upto(NC))

            def write_padding():
                for e in range(E):
                    for n in range(2 if e == E - 1 else 1):
                        sp.dma_start(rows_dram[bass.ds(end[e] + IR * n, IR), :].rearrange("(p j) c -> p j c", j=IT),
                                     pad_rows[:]).then_inc(pads_out, 16)
                sp.wait_ge(pads_out, 16 * (E + 1))

            with sp.If(end[0] < 2 * IR):
                write_padding()
            with sp.If(n_early < IR):
                load_rows(0)

            def late_padding(first):
                with sp.If(end[0] >= 2 * IR):
                    write_padding()

            def item(n):
                wait_apart(sp, t_done, upto(IT * n + IT))
                wait_apart(sp, next_kept, upto(n + 1))
                load_rows(n + 1)

            over_items(sp, 0, item, late_padding, lambda first: None, lambda first: load_next(1))
            with sp.Fori(1, E - 2) as e:
                over_items(sp, e, item, lambda first: None, lambda first: None, lambda first: load_next(e + 1))

            def load_gates(first):
                for q in range(SEQS):
                    sp.dma_start(gm[N * q:N * (q + 1), :, :],
                                 mods_v[q, :, G_M:G_M + C].partition_broadcast(N)).then_inc(ld_gm, 16)

            def load_low(first):
                sp.wait_ge(w1_ready, upto(E))
                sp.wait_ge(w1_rest, upto(2 * E))
                sp.wait_ge(w2_ready, upto(2 * E))
                sp.wait_ge(results_sent, upto(first))
                sp.dma_start(res_low[:], res_v[:, 0]).then_inc(ld_low, 16)

            over_items(sp, E - 2, item, load_gates)
            over_items(sp, E - 1, item, load_low)
            before_last = sp.value_load(per_expert[0:1, 1, E - 1:E], min_val=0, max_val=MOST)
            items = sp.value_load(per_expert[0:1, 0, E - 1:E], min_val=0, max_val=ITEMS)
            sp.wait_ge(results_sent, upto(items + before_last))

            def load_results(k):
                sp.dma_start(res[:, k % SLOTS], res_v[:, 1, FT * k:FT * (k + 1), :]).then_inc(ld_res[k % SLOTS], 16)

            for k in range(SLOTS):
                load_results(k)
            for k in range(NT // FT):
                sp.wait_ge(res_ready, k + 1)
                sp.dma_start(out_v[:, FT * k:FT * (k + 1), :],
                             x_sb[:, FT * k:FT * (k + 1), :]).then_inc(stored, 16)
                if k + SLOTS < NT // FT:
                    load_results(k + SLOTS)
            sp.wait_ge(stored, 16 * (NT // FT))

        @block.gpsimd
        def _(pool):
            nc.gpsimd.memset(ident[:], 0.0).then_inc(pool_chain, 1)
            pool.wait_ge(pool_chain, 1)
            nc.gpsimd.affine_select(out=ident[:], in_=ident[:], compare_op=ALU.not_equal, fill=1.0, base=0,
                                    pattern=[[-1, P]], channel_multiplier=1).then_inc(ident_ready, 1)
            nc.gpsimd.memset(bqk[:, 0, :], 0.0).then_inc(bias_set, 1)
            nc.gpsimd.memset(bqk[:, 1, :], 1.0).then_inc(bias_set, 1)
            nc.gpsimd.memset(wqk[:, 0:3].bitcast(FP32), 0.0).then_inc(pads_ready, 1)
            nc.gpsimd.memset(wqk[:, 3:5].bitcast(FP32), 0.0).then_inc(pads_ready, 1)
            nc.gpsimd.memset(minus_half[:], -0.5).then_inc(pool_chain, 1)
            nc.gpsimd.memset(va[:], 0.0).then_inc(consts_ready, 1)
            nc.gpsimd.memset(mpad[:], 0.0).then_inc(consts_ready, 1)
            start_counts(pool, y1_ready, y2_ready, rstd2_ready)
            nc.gpsimd.memset(tri[:], 1.0).then_inc(pool_chain, 1)
            pool.wait_ge(pool_chain, 3)
            start_counts(pool, rows_sent, results_sent)
            nc.gpsimd.affine_select(out=tri[:], in_=tri[:], compare_op=ALU.is_gt, fill=0.0, base=0,
                                    pattern=[[1, E], [-1, E]], channel_multiplier=0).then_inc(consts_ready, 1)
            nc.gpsimd.memset(ones[:], 1.0).then_inc(consts_ready, 1)
            nc.gpsimd.memset(before[:], 1.0).then_inc(router_chain, 1)
            nc.gpsimd.memset(pad_rows[:], 0.0).then_inc(router_chain, 1)
            pool.wait_ge(router_chain, 2)
            nc.gpsimd.affine_select(out=before[:], in_=before[:], compare_op=ALU.is_gt, fill=0.0, base=0,
                                    pattern=[[1, P]], channel_multiplier=-1).then_inc(consts_ready, 1)
            nc.gpsimd.iota(pad_rows[:, :, CX + E:XW].bitcast(I32), pattern=[[1, IT], [0, E]], base=TOP * T,
                           channel_multiplier=IT).then_inc(consts_ready, 1)
            nc.gpsimd.iota(token_i[:], pattern=[[P, NT]], base=0, channel_multiplier=1).then_inc(consts_ready, 1)
            nc.gpsimd.iota(first_i[:], pattern=[[REGION, E], [IR, ITEMS]], base=0,
                           channel_multiplier=0).then_inc(consts_ready, 1)
            nc.gpsimd.iota(number_i[:], pattern=[[1, ALL_ITEMS]], base=0, channel_multiplier=0).then_inc(consts_ready, 1)

            def rstd1(tiles, n, links):
                pool.wait_ge(var1_ready, n)
                nc.gpsimd.tensor_scalar(rstd[:, tiles], mv[:, tiles, 1], EPS, None, ALU.add).then_inc(pool_chain, 1)
                pool.wait_ge(pool_chain, links)
                nc.gpsimd.tensor_tensor(rstd[:, tiles], rstd[:, tiles], minus_half[:, tiles],
                                        ALU.pow).then_inc(rstd1_ready, 1)

            def modulate1(c, links, tiles=range(TPC)):
                pool.wait_ge(ld_mods1, 16 * SEQS * c + 16 * SEQS)
                for i in tiles:
                    y = y1[:, i, 0:C]
                    pool.wait_ge(y1_norm, upto(TPC * c + i + 1))
                    nc.gpsimd.tensor_tensor(y, y, mods1[:, i, 1, :], ALU.mult).then_inc(pool_chain, 1)
                    pool.wait_ge(pool_chain, links + 2 * i + 1)
                    nc.gpsimd.tensor_tensor(y1[:, i, C:CX].rearrange("p (r n) -> p r n", n=CR),
                                            rep_last(y, REP - 1), rep_last(mods1[:, i, 0, :], REP - 1),
                                            ALU.add).then_inc(pool_chain, 1)
                    pool.wait_ge(pool_chain, links + 2 * i + 2)
                    nc.gpsimd.tensor_tensor(y, y, mods1[:, i, 0, :], ALU.add).then_inc(y1_ready, 1)

            def tile_norm(t, c, links):
                wait_apart(pool, var2_ready, upto(TPC * c + t + 1))
                nc.gpsimd.tensor_scalar(rstd2[:, t % 2:t % 2 + 1], mv2[:, t % 2, 1:2], EPS, None,
                                        ALU.add).then_inc(pool_chain, 1)
                pool.wait_ge(pool_chain, links)
                nc.gpsimd.tensor_tensor(rstd2[:, t % 2:t % 2 + 1], rstd2[:, t % 2:t % 2 + 1], minus_half[:, 0:1],
                                        ALU.pow).then_inc(rstd2_ready, 1)
                pool.wait_ge(y2_norm, upto(TPC * c + t + 1))
                y = y2[:, t, 0:C]
                nc.gpsimd.tensor_tensor(y, y, mods2[:, t, 2, :], ALU.mult).then_inc(pool_chain, 1)
                pool.wait_ge(pool_chain, links + 1)
                nc.gpsimd.tensor_tensor(y2[:, t, C:CX].rearrange("p (r n) -> p r n", n=CR),
                                        rep_last(y, REP - 1), rep_last(mods2[:, t, 1, :], REP - 1),
                                        ALU.add).then_inc(pool_chain, 1)
                pool.wait_ge(pool_chain, links + 2)
                nc.gpsimd.tensor_tensor(y, y, mods2[:, t, 1, :], ALU.add).then_inc(y2_ready, 1)

            def chunk(c, more):
                links = BEFORE + LINKS * c
                pool.wait_ge(ld_mods2, 16 * SEQS * c + 16 * SEQS)
                if more:
                    modulate1(c + 1, links)
                    links += 2 * TPC
                for t in range(TPC):
                    tile_norm(t, c, links + 1)
                    links += 3
                    if t == TPC - 1:
                        send_rows(0, c)
                send_rows(1, c)
                pool.wait_ge(rows_out, ROWS_OUT * c + ROWS_OUT)
                pool.sem_inc(rows_sent, 1)

            def send_rows(h, c):
                wait_apart(pool, route_ready, upto(2 * c + h + 1))
                for i in (2 * h, 2 * h + 1):
                    for choice in range(TOP):
                        nc.gpsimd.indirect_dma_start(
                            rows_dram, bass.IndirectOffsetOnAxis(ap=places[:, choice, i, 0:1], axis=0), y2[:, i, :],
                            None).then_inc(rows_out, 16)

            LINKS = 5 * TPC
            BEFORE = 5 + TPC
            rstd1(slice(0, TPC), 1, 4)
            modulate1(0, 4, range(TPC // 2))
            pool.wait_ge(y1_other, TPC // 2)
            pool.wait_ge(t1_done, upto(TPC // 2))
            pool.sem_inc(y1_ready, TPC // 2)
            for weight_split in (wqk_ready, wv_ready, wp_ready):
                pool.wait_ge(weight_split, 1)
            nc.gpsimd.memset(kblk[:], 0.0).then_inc(kblk_zero, 1)
            rstd1(slice(TPC, NT), 2, BEFORE)
            with pool.Fori(0, NC - 1) as c:
                chunk(c, True)
            chunk(NC - 1, False)

            def item(n):
                wait_apart(pool, y_ready, upto(n + 1))
                for i in range(IT):
                    nc.gpsimd.indirect_dma_start(
                        res_dram, bass.IndirectOffsetOnAxis(ap=item_to[:, i:i + 1], axis=0), y_out[:, i, :],
                        None).then_inc(scattered, 16)
                wait_apart(pool, scattered, 16 * IT * n + 16 * IT)
                pool.sem_inc(results_sent, 1)

            w1_in = w1_raw[:].rearrange("p k (q j) -> p k j q", j=HJ)

            def expert(e, q):
                def rest_lo(first):
                    wait_apart(pool, w1hi, upto(KT * e + 2 * KT))
                    for r in (1, 3):
                        rr = slice(CR * r, CR * (r + 1))
                        nc.gpsimd.tensor_tensor(w1s[1 - q][rr, REST], w1_in[rr, KF], w1s[1 - q][rr, REST],
                                                ALU.subtract).then_inc(w1_rest, 1)
                    wait_apart(pool, w1_rest, upto(2 * e + 4))

                def w2_lo(first):
                    wait_apart(pool, w2hi, upto(e + 2))
                    nc.gpsimd.tensor_tensor(w2s[1 - q][:, 1, :POOL_J], w2_raw[:, :POOL_J], w2s[1 - q][:, 0, :POOL_J],
                                            ALU.subtract).then_inc(w2_ready, 1)

                over_items(pool, e, item, rest_lo, w2_lo)

            def add_low(c):
                if c == 0:
                    pool.wait_ge(ld_low, 16)
                    pool.wait_ge(ld_gm, 16 * SEQS)
                tiles = slice(TPC * c, TPC * (c + 1))
                nc.gpsimd.tensor_tensor(res_low[:, tiles], res_low[:, tiles], gm[:, tiles], ALU.mult).then_inc(low_gated, 1)
                pool.wait_ge(low_gated, c + 1)
                nc.gpsimd.tensor_tensor(x_sb[:, tiles], x_sb[:, tiles], res_low[:, tiles], ALU.add).then_inc(low_added, 1)

            with pool.Fori(0, E // 2 - 1) as e:
                expert(2 * e, 0)
                expert(2 * e + 1, 1)
            expert(E - 2, 0)
            over_items(pool, E - 1, item, *[lambda first, c=c: add_low(c) for c in range(NC)])

        @block.scalar
        def _(act):
            load_split(act, wqkv_raw, w_qkv, ld_qkv)
            act.wait_ge(ld_c, 16)
            nc.scalar.activation(c_sb[:, 1, :], c_sb[:, 0, :], ACT.Exp, scale=-1.0).then_inc(e_ready, 1)
            act.dma_start(bv_b[:], b_qkv[2 * C:3 * C].partition_broadcast(P)).then_inc(ld_small, 16)
            act.dma_start(bp_b[:], b_proj.partition_broadcast(P)).then_inc(ld_small, 16)
            act.wait_ge(bias_set, 2)
            for qk in range(2):
                for i in range(4):
                    act.dma_start(bqk[HW * i:HW * i + HD, qk, :],
                                  b_qkv[qk * C:(qk + 1) * C].rearrange("(g i d) -> i d g", i=4, d=HD)[i],
                                  allow_slow_non_contiguous=True).then_inc(ld_bqk, 16)
            act.dma_start(wg[:, 0:KF, :], w_gate[0:KF * P, :].rearrange("(k p) n -> p k n", p=P)).then_inc(ld_small, 16)
            act.dma_start(wg[0:CR, KF, :], rows_rep(w_gate)).then_inc(ld_small, 16)
            load_split(act, wp_raw, w_proj, ld_wp)
            for e in range(E):
                act.dma_start(b2_b[:, e, :], b2[e, :].partition_broadcast(P)).then_inc(ld_b2, 16)
            act.dma_start(b1_sb[:], b1.rearrange("e (p j) -> p e j", j=HJ)).then_inc(ld_b1, 16)
            def copy(dst, src):
                return nc.scalar.activation(dst, src, ACT.Copy)

            def hi_of_tile(dst, bank):
                return copy(dst, ps[:, bank, 0:KT * P].rearrange("p (k t) -> p k t", t=P))

            def job(name, c, bank):
                kind, i = name
                if kind == "T1":
                    act.wait_ge(t1_done, upto(TPC * c + i + 1))
                    hi_of_tile(h1[:, 0:KT, P * i:P * (i + 1)], bank).then_inc(h1_hi, 1)
                elif kind == "QK":
                    qk, g = (1, i) if i < HG else (0, i - HG)
                    if i == 0:
                        act.wait_ge(bqk_ready, 1)
                        act.wait_ge(st_done, upto(TPC * c))
                    act.wait_ge(qk_done, upto(2 * HG * c + i + 1))
                    bias = bqk[:, qk, g:g + 1]
                    if qk:
                        nc.scalar.activation(kT[:, g, :], ps[:, bank, :], ACT.Identity, bias=bias,
                                             scale=1.0).then_inc(qk_read, 1)
                        act.wait_ge(kblk_ready, upto(HG * c))
                        act.wait_ge(qk_read, upto(2 * HG * c + i + 1))
                        copy(kTb[:, g, :], kT[:, g, :]).then_inc(kTb_ready, 1)
                    else:
                        nc.scalar.activation(qT[:, g, :], ps[:, bank, :], ACT.Identity, bias=bias,
                                             scale=SCALE).then_inc(qk_read, 1)
                        act.wait_ge(qk_read, upto(2 * HG * c + i + 1))
                        copy(qTb[:, g, :], qT[:, g, :]).then_inc(qTb_ready, 1)
                elif kind == "OT":
                    act.wait_ge(ot_done, upto(TPC * c + i + 1))
                    act.wait_ge(pj_done, upto(TPC * c + max(i - 1, 0)))
                    hi_of_tile(ox[:, i % 2, 0:KT], bank).then_inc(ox_hi, 1)
                elif kind == "T2":
                    act.wait_ge(t2_done, upto(TPC * c + i + 1))
                    act.wait_ge(lg_done, upto(TPC * c + max(i - 1, 0)))
                    copy(yT[:, i % 2], ps[:, bank, 0:KT * P].rearrange("p (k t) -> p k t", t=P)
                         ).then_inc(yT_ready, 1)
                elif kind == "RT":
                    act.wait_ge(rmax_ready, upto(2 * c + i + 1))
                    nc.scalar.activation(r_exp[:], r_exp[:], ACT.Exp).then_inc(rexp_ready, 1)

            def softmax(t, c):
                act.wait_ge(st_done, upto(TPC * c + t + 1))
                act.wait_ge(pv_done, upto(TPC * c + t))
                nc.scalar.activation(pT[:].rearrange("p i g q -> p i (g q)"), ps[:, 4:8, 0:HG * N],
                                     ACT.Exp).then_inc(exp_done, 1)

            w1_in = w1_raw[:].rearrange("p k (q j) -> p k j q", j=HJ)

            def w1_hi(e, q):
                wait_apart(act, ld_w1, SPLIT_LD * e + SPLIT_LD)
                for k in range(KT):
                    nc.scalar.activation(w1s[q][:, k], w1_in[:, k], ACT.Copy).then_inc(w1hi, 1)

            def w2_hi(e, q):
                wait_apart(act, ld_w2, 16 * e + 16)
                nc.scalar.activation(w2s[q][:, 0], w2_raw[:], ACT.Copy).then_inc(w2hi, 1)

            start_counts(act, kTb_ready, qTb_ready, h1_hi, qk_read, ox_hi, yT_ready, exp_done, rexp_ready,
                         gelu_done, xT_hi, w1hi, w2hi)
            for name, c, bank in first_jobs():
                job(name, c, bank)

            def chunk(c, more):
                for what, name, k, bank in schedule(c, more):
                    if what == "scores":
                        softmax(name, c)
                    elif what == "job":
                        job(name, k, bank)
                    elif name == "w1 hi":
                        w1_hi(0, 0)
                    elif name == "w2 hi":
                        w2_hi(0, 0)

            with act.Fori(0, NC - 1) as c:
                chunk(c, True)
            chunk(NC - 1, False)

            def prepare(n):
                for i in range(IT):
                    wait_apart(act, t_done, upto(IT * n + i + 1))
                    copy(xT[:, 0:KT, P * i:P * (i + 1)],
                         ps[:, 6 + i, 0:KT * P].rearrange("p (k t) -> p k t", t=P)).then_inc(xT_hi, 1)

            def expert(e, q):
                def item(n):
                    for j in range(HJ):
                        act.wait_ge(s1_done, upto(HJ * n + min(j // 2 * 2 + 2, HJ)))
                        wait_apart(act, h_ready, upto(HJ * n + max(j - 1, 0)))
                        nc.scalar.activation(h32[:, j % 2, :], unit_slot(j), ACT.Gelu_apprx_tanh,
                                             bias=b1_sb[:, bass.ds(e, 1), j:j + 1].rearrange("p a b -> p (a b)"),
                                             ).then_inc(gelu_done, 1)
                    prepare(n + 1)

                def next_w1(first):
                    with act.If(e < E - 1):
                        wait_apart(act, s2_done, upto(IT * first))
                        w1_hi(e + 1, 1 - q)

                def next_w2(first):
                    with act.If(e < E - 1):
                        w2_hi(e + 1, 1 - q)

                over_items(act, e, item, next_w1, next_w2)

            act.wait_ge(ld_b1, 16)
            prepare(0)
            with act.Fori(0, E // 2) as e:
                expert(2 * e, 0)
                expert(2 * e + 1, 1)

        @block.vector
        def _(dve):
            V = nc.vector
            chain = [0, 0]

            def link(ins, base=0):
                chain[0] += 1
                ins.then_inc(dve_chain, 1)
                dve.wait_ge(dve_chain, base + chain[0])

            def split_weight(dst, raw, s):
                for k in range(KT):
                    last = V.tensor_copy(dst(k), raw(k))
                link(last)
                for k in range(KF):
                    V.tensor_tensor(dst(LO + k), raw(k), dst(k), ALU.subtract)
                for r in (1, 3):
                    rr = slice(CR * r, CR * (r + 1))
                    last = V.tensor_tensor(dst(REST)[rr], raw(KF)[rr], dst(REST)[rr], ALU.subtract)
                last.then_inc(s, 1)

            V.memset(sT[CR:CR + 1, KF, :], 1.0).then_inc(ident_ready, 1)
            dve.wait_ge(e_ready, 1)
            link(V.tensor_scalar(c_sb[:, 1, :], c_sb[:, 1, :], 1.0, None, ALU.add))
            link(V.reciprocal(c_sb[:, 2, :], c_sb[:, 1, :]))
            V.tensor_tensor(c_sb[:, 2, :], c_sb[:, 2, :], c_sb[:, 0, :], ALU.mult).then_inc(s_ready, 1)
            dve.wait_ge(sT_done, 1)
            V.tensor_copy(sT[:, 0:KF, :], ps[:, 0, 0:KF * B].rearrange("p (k b) -> p k b", b=B))
            V.tensor_copy(sT[0:CR, KF, :], ps[0:CR, 0, KF * B:KT * B]).then_inc(sT_ready, 1)

            def stats1(tiles):
                for t in tiles:
                    last = V.bn_stats(stats[:, t, :], x_sb[:, t, :])
                link(last)
                for t in tiles:
                    last = V.bn_aggr(mv[:, t, :], stats[:, t, :])
                last.then_inc(var1_ready, 1)

            def modulation(half):
                dve.wait_ge(mod_done, half + 1)
                cols = slice(2 * MODN * half, 2 * MODN * (half + 1))
                link(V.tensor_copy(mod_sb[:, cols].rearrange("b (g n) -> b g n", n=MODN),
                                   ps[0:B, 4 + 2 * half:6 + 2 * half, 0:MODN]))
                scale = mod_sb[:, (SC_A, SC_M)[half]:(SC_A, SC_M)[half] + C]
                V.tensor_scalar(scale, scale, 1.0, None, ALU.add).then_inc(mod_ready, 1)

            dve.wait_ge(ld_x0, 16)
            stats1(range(TPC))
            dve.wait_ge(ld_qkv, SPLIT_LD)
            dve.wait_ge(pads_ready, 2)
            qk_raw = wqkv_raw[:, :, 0:2 * C].rearrange("p k (h d) -> p k h d", d=HD)
            split_weight(lambda s: wqk[:, s, :, 0:HD], lambda k: qk_raw[:, k], wqk_ready)
            modulation(0)
            split_weight(lambda s: wv[:, s, :], lambda k: wqkv_raw[:, k, 2 * C:3 * C], wv_ready)
            dve.wait_ge(ld_bqk, 8 * 16)
            V.tensor_scalar(bqk[:, 0, :], bqk[:, 0, :], SCALE, None, ALU.mult).then_inc(bqk_ready, 1)

            def rest_of_start():
                dve.wait_ge(ld_wp, SPLIT_LD)
                split_weight(lambda s: wp[:, s, :], lambda k: wp_raw[:, k, :], wp_ready)
                modulation(1)
                dve.wait_ge(ld_x, 16 * (NC - 1))
                stats1(range(TPC, NT))
                dve.wait_ge(ld_small, 4 * 16)

            dve.wait_ge(consts_ready, 9)
            for q in range(SEQS):
                V.memset(va[N * q:N * (q + 1), :, :, q, HD], 1.0)
            dve.wait_ge(rstd1_ready, 1)
            start_counts(dve, kblk_ready, y1_norm, h1_ready, v_ready, red_done, add_done, o_ready, ox_ready, pj_read,
                         x2_ready, var2_ready, y2_norm, lg_ready, rmax_ready, sel_ready, rt_read, route_ready,
                         h_ready, xT_ready, next_kept, y_read, y_ready, w1_ready, w1_rest, w2_ready)
            V.tensor_copy(token[:], token_i[:])
            V.tensor_copy(i_number[:], number_i[:])
            link(V.tensor_copy(i_first[:], first_i[:]))
            link(V.tensor_copy(count[:], i_first[:, :, 0]))

            def x_tile(c, i):
                return x_sb[:, bass.ds(TPC * c + i, 1), :].rearrange("p a c -> p (a c)")

            def norm1(c):
                dve.wait_ge(t1_done, upto(TPC * c))
                for i in range(TPC):
                    V.tensor_scalar(y1[:, i, 0:C], x_tile(c, i),
                                    mv[:, bass.ds(TPC * c + i, 1), 0:1].rearrange("p a b -> p (a b)"),
                                    rstd[:, bass.ds(TPC * c + i, 1)], ALU.subtract, ALU.mult).then_inc(y1_norm, 1)

            def lo_of_tile(dst, src):
                V.tensor_tensor(dst[:, LO:LO + KF], src[:, 0:KF], dst[:, 0:KF], ALU.subtract)
                lo = slice(2 * CR, P)
                return V.tensor_tensor(dst[lo, REST], src[lo, KF], dst[lo, REST], ALU.subtract)

            def neg_max(t, c):
                dve.wait_ge(mx_done, upto(TPC * c + t + 1))
                dve.wait_ge(mt_done, upto(TPC * c + t))
                V.tensor_reduce(mpad[:].rearrange("p g (i w) -> p g i w", w=HW)[:, :, :, HD],
                                ps[:, 0:2, :].rearrange("p b (g i k) -> p (b g) i k", i=4, k=N),
                                AX.X, ALU.max, negate=True).then_inc(red_done, 1)

            def add_max(t, c):
                dve.wait_ge(mt_done, upto(TPC * c + t + 1))
                q = qT[:, :, P * (t % TPC):P * (t % TPC + 1)]
                V.tensor_tensor(q, q, ps[:, 0, :].rearrange("p (g q) -> p g q", q=P), ALU.add).then_inc(add_done, 1)

            def normalise(t, c, base):
                dve.wait_ge(pv_done, upto(TPC * c + t + 1))
                o_ps = ps[0:N, 4:6, 0:NH // 2 * SEQS * VW].rearrange("p b (h q d) -> p b h q d", q=SEQS, d=VW)
                o_heads = o_sb[:, t % 2, 0:C].rearrange("p (b h d) -> p b h d", b=2, d=HD)
                for q in range(SEQS):
                    last = V.reciprocal(rden[:, :, :, q], o_ps[:, :, :, q, HD])
                link(last, base)
                for q in range(SEQS):
                    last = V.tensor_tensor(o_heads[N * q:N * (q + 1)], o_ps[:, :, :, q, 0:HD],
                                           rden[:, :, :, q].unsqueeze(3).broadcast_to([N, 2, NH // 2, HD]), ALU.mult)
                link(last, base)
                V.tensor_copy(o_sb[:, t % 2, C:CX].rearrange("p (r n) -> p r n", n=CR),
                              rep_last(o_sb[:, t % 2, :], REP - 1)).then_inc(o_ready, 1)

            def norm2(i, c):
                wait_apart(dve, rstd2_ready, upto(TPC * c + i + 1))
                dve.wait_ge(rows_sent, upto(c))
                V.tensor_scalar(y2[:, i, 0:C], x_tile(c, i), mv2[:, i % 2, 0:1], rstd2[:, i % 2:i % 2 + 1],
                                ALU.subtract, ALU.mult).then_inc(y2_norm, 1)

            def job(name, c, bank, base):
                kind, i = name
                n = upto(TPC * c + i + 1)
                if kind == "T1":
                    dve.wait_ge(h1_hi, n)
                    lo_of_tile(h1[:, :, P * i:P * (i + 1)],
                               ps[:, bank, 0:KT * P].rearrange("p (k t) -> p k t", t=P)).then_inc(h1_ready, 1)
                elif kind == "QK":
                    if i == 0:
                        dve.wait_ge(mx_done, upto(TPC * c))
                    dve.wait_ge(kTb_ready, upto(HG * c + i + 1))
                    for h in range(4):
                        rows = slice(HW * h, HW * (h + 1))
                        last = V.tensor_copy(kblk[rows, i, :, h, :], kTb[rows, i].rearrange("p (b n) -> p b n", n=N))
                    last.then_inc(kblk_ready, 1)
                elif kind == "V":
                    dve.wait_ge(v_done, n)
                    for q in range(SEQS):
                        rows = slice(N * q, N * (q + 1))
                        last = V.tensor_tensor(va[rows, i, :, q, 0:HD],
                                               ps[rows, bank, 0:C].rearrange("p (h d) -> p h d", d=HD),
                                               bv_b[rows].rearrange("p (h d) -> p h d", d=HD), ALU.add)
                    last.then_inc(v_ready, 1)
                elif kind == "OT":
                    dve.wait_ge(ox_hi, n)
                    lo_of_tile(ox[:, i % 2], ps[:, bank, 0:KT * P].rearrange("p (k t) -> p k t", t=P)
                               ).then_inc(ox_ready, 1)
                elif kind == "PJ":
                    dve.wait_ge(pj_done, n)
                    V.tensor_tensor(pj[:, i % 2, :], ps[:, bank, 0:C], bp_b[:], ALU.add).then_inc(pj_read, 1)
                elif kind == "LG":
                    dve.wait_ge(lg_done, n)
                    V.tensor_copy(logits[:, i, :], ps[:, bank, 0:E]).then_inc(lg_ready, 1)
                elif kind == "RT":
                    route(i, c, bank, base)

            def residual(i, c, base):
                n = upto(TPC * c + i + 1)
                dve.wait_ge(ld_mods2, 16 * SEQS * c + 16 * SEQS)
                dve.wait_ge(pj_read, n)
                link(V.tensor_tensor(pj[:, i % 2, :], pj[:, i % 2, :], mods2[:, i, 0, :], ALU.mult), base)
                V.tensor_tensor(x_tile(c, i), x_tile(c, i), pj[:, i % 2, :], ALU.add).then_inc(x2_ready, 1)
                wait_apart(dve, x2_ready, n)
                link(V.bn_stats(stats2[:, i % 2, :], x_tile(c, i)), base)
                dve.sem_inc(passed, 1)
                V.bn_aggr(mv2[:, i % 2, :], stats2[:, i % 2, :]).then_inc(var2_ready, 1)

            def select(h, c, base):
                n = upto(2 * c + h + 1)
                own = logits[:, 2 * h:2 * h + 2, :]
                l_j = own.unsqueeze(2).broadcast_to([P, 2, E, E])
                l_e = own.unsqueeze(3).broadcast_to([P, 2, E, E])
                wait_apart(dve, lg_ready, upto(TPC * c + 2 * h + 2))
                dve.wait_ge(route_ready, upto(2 * c + h))
                V.tensor_tensor(r_gt[:], l_j, l_e, ALU.is_gt)
                V.tensor_reduce(r_max[:], own, AX.X, ALU.max)
                link(V.tensor_tensor(r_eq[:], l_j, l_e, ALU.is_equal), base)
                V.tensor_tensor(r_exp[:], own, r_max[:].unsqueeze(2).broadcast_to([P, 2, E]),
                                ALU.subtract).then_inc(rmax_ready, 1)
                eq16 = r_eq[:].rearrange("p t e j -> p t (e j)")
                tri16 = tri[:].rearrange("p e j -> p (e j)").unsqueeze(1).broadcast_to([P, 2, E * E])
                link(V.tensor_tensor(eq16, eq16, tri16, ALU.mult), base)
                link(V.tensor_tensor(r_gt[:], r_gt[:], r_eq[:], ALU.add), base)
                link(V.tensor_reduce(r_sel[:], r_gt[:], AX.X, ALU.add), base)
                V.tensor_scalar(r_sel[:], r_sel[:], 1.5, None, ALU.is_lt).then_inc(sel_ready, 1)

            def route(h, c, bank, base):
                n = upto(2 * c + h + 1)
                dve.wait_ge(sel_ready, n)
                dve.wait_ge(rt_done, n)
                V.tensor_tensor(r_pos[:], ps[:, bank, 0:2 * E].rearrange("p (t e) -> p t e", e=E),
                                count[:].unsqueeze(1).broadcast_to([P, 2, E]), ALU.add)
                wait_apart(dve, rexp_ready, n)
                link(V.tensor_tensor(r_exp[:], r_exp[:], r_sel[:], ALU.mult), base)
                V.tensor_tensor(count[:], count[:], ps[:, bank, 2 * E:3 * E], ALU.add).then_inc(rt_read, 1)
                V.tensor_reduce(r_sum[:], r_exp[:], AX.X, ALU.add)
                V.scalar_tensor_tensor(r_masked[:, 0], r_pos[:], -FAR, r_sel[:], ALU.add, ALU.mult)
                link(V.tensor_tensor(r_masked[:, 1], r_pos[:], r_sel[:], ALU.mult), base)
                V.reciprocal(r_sum[:], r_sum[:])
                V.tensor_reduce(r_ends[:, 0], r_masked[:, 0], AX.X, ALU.min)
                link(V.tensor_reduce(r_ends[:, 1], r_masked[:, 1], AX.X, ALU.max), base)
                V.tensor_tensor(y2[:, 2 * h:2 * h + 2, CX:CX + E], r_exp[:],
                                r_sum[:].unsqueeze(2).broadcast_to([P, 2, E]), ALU.mult)
                V.tensor_scalar(places[:, 0, 2 * h:2 * h + 2, 0], r_ends[:, 0], FAR, None, ALU.add)
                V.tensor_copy(places[:, 1, 2 * h:2 * h + 2, 0], r_ends[:, 1])
                link(V.tensor_tensor(r_pos[:], r_pos[:], r_ends[:, 1].unsqueeze(2).broadcast_to([P, 2, E]),
                                     ALU.is_equal), base)
                V.scalar_tensor_tensor(y2[:, 2 * h:2 * h + 2, CX + E:XW].bitcast(I32), r_pos[:], float(T),
                                       token[:, bass.ds(TPC * c + 2 * h, 2)].unsqueeze(2).broadcast_to([P, 2, E]),
                                       ALU.mult, ALU.add).then_inc(route_ready, 1)

            w1_in = w1_raw[:].rearrange("p k (q j) -> p k j q", j=HJ)

            def w2_lo(e, q):
                dve.wait_ge(w2hi, upto(e + 1))
                V.tensor_tensor(w2s[q][:, 1, POOL_J:], w2_raw[:, POOL_J:], w2s[q][:, 0, POOL_J:],
                                ALU.subtract).then_inc(w2_ready, 1)

            def w1_lo(e, q):
                dve.wait_ge(w1hi, upto(KT * e + KF))
                for k in range(KF):
                    last = V.tensor_tensor(w1s[q][:, LO + k], w1_in[:, k], w1s[q][:, k], ALU.subtract)
                last.then_inc(w1_ready, 1)

            def first_weights(part):
                if part == "w1 lo":
                    w1_lo(0, 0)
                elif part == "w1 rest":
                    dve.wait_ge(w1hi, upto(KT))
                    for r in (1, 3):
                        rr = slice(CR * r, CR * (r + 1))
                        V.tensor_tensor(w1s[0][rr, REST], w1_in[rr, KF], w1s[0][rr, REST],
                                        ALU.subtract).then_inc(w1_rest, 1)
                elif part == "w2 lo":
                    w2_lo(0, 0)
                    V.tensor_tensor(w2s[0][:, 1, :POOL_J], w2_raw[:, :POOL_J], w2s[0][:, 0, :POOL_J],
                                    ALU.subtract).then_inc(w2_ready, 1)

            def chunk(c, more, base):
                if more:
                    norm1(c + 1)
                for what, name, k, bank in schedule(c, more):
                    if what == "max":
                        neg_max(name, c)
                    elif what == "move":
                        add_max(name, c)
                    elif what == "values 1":
                        normalise(name, c, base)
                    elif what == "residual":
                        residual(name, c, base)
                    elif what == "norm":
                        norm2(name, c)
                    elif what == "select":
                        select(name, c, base)
                    elif what == "weights":
                        first_weights(name)
                    elif what == "job" and not (name[0] == "QK" and name[1] >= HG):
                        job(name, k, bank, base)

            norm1(0)
            dve.wait_ge(ld_mods1, 16 * SEQS)
            for i in range(TPC // 2, TPC):
                y = y1[:, i, 0:C]
                dve.wait_ge(y1_norm, upto(i + 1))
                link(V.tensor_tensor(y, y, mods1[:, i, 1, :], ALU.mult))
                link(V.tensor_tensor(y1[:, i, C:CX].rearrange("p (r n) -> p r n", n=CR), rep_last(y, REP - 1),
                                     rep_last(mods1[:, i, 0, :], REP - 1), ALU.add))
                V.tensor_tensor(y, y, mods1[:, i, 0, :], ALU.add).then_inc(y1_other, 1)
            for name, c, bank in first_jobs():
                if name == ("QK", 0):
                    rest_of_start()
                    dve.wait_ge(kblk_zero, 1)
                if not (name[0] == "QK" and name[1] >= HG):
                    job(name, c, bank, 0)
            neg_max(0, 0)
            add_max(0, 0)
            dve.wait_ge(rstd1_ready, 2)
            LINKS = 4 * TPC + 2 * 8
            before = chain[0]
            with dve.Fori(0, NC - 1) as c:
                chunk(c, True, LINKS * c)
                assert chain[0] - before == LINKS, chain[0] - before
            chain[0] = before + LINKS * (NC - 1)
            V.tensor_copy(early[:], count[:, 0:1]).then_inc(early_ready, 1)
            chunk(NC - 1, False, 0)

            link(V.tensor_tensor(i_in[:], i_first[:], count[:].unsqueeze(2).broadcast_to([P, E, ITEMS]), ALU.is_lt))
            link(V.tensor_reduce(i_n[:], i_in[:], AX.X, ALU.add))
            V.tensor_scalar(i_skip[:], i_n[:], -float(IR), float(REGION), ALU.mult, ALU.add)
            link(V.tensor_tensor(i_tri[:], tri[:], i_n[:].unsqueeze(1).broadcast_to([P, E, E]), ALU.mult))
            link(V.tensor_reduce(i_before[:], i_tri[:], AX.X, ALU.add))
            link(V.tensor_tensor(i_from[:], i_number[:].unsqueeze(2).broadcast_to([P, ALL_ITEMS, E - 1]),
                                 i_before[:, 1:E].unsqueeze(1).broadcast_to([P, ALL_ITEMS, E - 1]), ALU.is_ge))
            link(V.tensor_tensor(i_from[:], i_from[:], i_skip[:, 0:E - 1].unsqueeze(1).broadcast_to(
                [P, ALL_ITEMS, E - 1]), ALU.mult))
            link(V.tensor_reduce(i_row[:], i_from[:], AX.X, ALU.add))
            V.scalar_tensor_tensor(item_row[:], i_number[:], float(IR), i_row[:], ALU.mult, ALU.add)
            V.tensor_copy(per_expert[:, 0], i_n[:])
            V.tensor_copy(per_expert[:, 1], i_before[:])
            link(V.tensor_copy(per_expert[:, 2], count[:]))
            dve.sem_inc(items_ready, 1)

            def prepare(n):
                for i in range(IT):
                    dve.wait_ge(xT_hi, upto(IT * n + i + 1))
                    lo_of_tile(xT[:, :, P * i:P * (i + 1)],
                               ps[:, 6 + i, 0:KT * P].rearrange("p (k t) -> p k t", t=P)).then_inc(xT_ready, 1)

            def keep_next(n):
                wait_apart(dve, ld_rows, 16 * n + 16)
                V.tensor_copy(next_w[:], xr[:, :, CX:XW]).then_inc(next_kept, 1)

            def expert(e, q):
                def item(n):
                    dve.wait_ge(s2_done, upto(IT * n))
                    for j in range(HJ):
                        dve.wait_ge(gelu_done, upto(HJ * n + j + 1))
                        V.tensor_copy(hs[:, 0, j, :], h32[:, j % 2, :]).then_inc(h_hi, 1)
                        dve.wait_ge(h_hi, upto(HJ * n + j + 1))
                        V.tensor_tensor(hs[:, 1, j, :], h32[:, j % 2, :], hs[:, 0, j, :],
                                        ALU.subtract).then_inc(h_ready, 1)
                    wait_apart(dve, results_sent, upto(n))
                    wait_apart(dve, next_kept, upto(n + 1))
                    V.tensor_copy(item_w[:], next_w[:, :, bass.ds(e, 1)].rearrange("p i a -> p (i a)"))
                    V.tensor_copy(item_to[:], next_w[:, :, bass.ds(E + e, 1)].rearrange(
                        "p i a -> p (i a)").bitcast(I32)).then_inc(w_kept, 1)
                    wait_apart(dve, w_kept, upto(n + 1))
                    keep_next(n + 1)
                    prepare(n + 1)
                    for i in range(IT):
                        dve.wait_ge(s2_done, upto(IT * n + i + 1))
                        V.tensor_tensor(y_add[:, i, :], ps[:, 4 + i, 0:C],
                                        b2_b[:, bass.ds(e, 1), :].rearrange("p a c -> p (a c)"), ALU.add
                                        ).then_inc(y_read, 1)
                    wait_apart(dve, y_read, upto(IT * n + IT))
                    for i in range(IT):
                        ins = V.tensor_scalar(y_out[:, i, :], y_add[:, i, :], item_w[:, i:i + 1], None, ALU.mult)
                    ins.then_inc(y_ready, 1)

                def next_w1(first):
                    with dve.If(e < E - 1):
                        w1_lo(e + 1, 1 - q)

                def next_w2(first):
                    with dve.If(e < E - 1):
                        w2_lo(e + 1, 1 - q)

                over_items(dve, e, item, next_w1, next_w2)

            start_counts(dve, h_hi, w_kept)
            keep_next(0)
            prepare(0)
            dve.wait_ge(ld_b2, 16 * E)
            with dve.Fori(0, E // 2) as e:
                expert(2 * e, 0)
                expert(2 * e + 1, 1)
            dve.wait_ge(low_added, NC)
            for k in range(NT // FT):
                tiles = slice(FT * k, FT * (k + 1))
                dve.wait_ge(ld_res[k % SLOTS], 16 * (k // SLOTS + 1))
                link(V.tensor_tensor(res[:, k % SLOTS], res[:, k % SLOTS], gm[:, tiles], ALU.mult))
                V.tensor_tensor(x_sb[:, tiles, :], x_sb[:, tiles, :], res[:, k % SLOTS], ALU.add).then_inc(res_ready, 1)

        @block.tensor
        def _(pe):
            M = nc.tensor.matmul

            def split_matmul(out_ap, stat, mov):
                for n, (a, b) in enumerate(PAIRS):
                    last = M(out_ap, stat(a), mov(b), start=(n == 0), stop=(n == len(PAIRS) - 1))
                return last

            pe.wait_ge(ident_ready, 2)
            pe.wait_ge(s_ready, 1)
            for k in range(KT):
                n = P if k < KF else CR
                last = nc.tensor.transpose(ps[0:n, 0, B * k:B * (k + 1)], c_sb[:, 2, P * k:P * k + n], ident[0:B, 0:B])
            last.then_inc(sT_done, 1)
            pe.wait_ge(sT_ready, 1)
            pe.wait_ge(ld_ada, 3 * 16)
            for g in range(4):
                cols = slice(MODN * g, MODN * (g + 1))
                o = ps[0:B, 4 + g, 0:MODN]
                for k in range(KT):
                    n = P if k < KF else CR + 1
                    last = M(o, sT[0:n, k, :], w_ada_sb[0:n, k, cols], start=(k == 0), stop=(k == KF))
                if g % 2 == 1:
                    last.then_inc(mod_done, 1)

            def transpose_tile(rows, bank):
                for k in range(KT):
                    last = nc.tensor.transpose(ps[:, bank, P * k:P * (k + 1)], rows[:, P * k:P * (k + 1)], ident[:])
                return last

            def wait_read(name, c):
                kind, i = name
                reader, per_chunk = {"T1": (h1_ready, TPC), "QK": (qk_read, 2 * HG), "V": (v_ready, TPC),
                                     "OT": (ox_ready, TPC), "PJ": (pj_read, TPC), "T2": (yT_ready, TPC),
                                     "LG": (lg_ready, TPC), "RT": (rt_read, 2)}[kind]
                pe.wait_ge(reader, upto(per_chunk * c + i + 1))

            def job(name, c, bank):
                kind, i = name
                n = upto(TPC * c + i + 1)
                if kind == "T1":
                    if isinstance(c, int) and c == 0 and i >= TPC // 2:
                        pe.wait_ge(y1_other, i - TPC // 2 + 1)
                    else:
                        pe.wait_ge(y1_ready, n)
                    transpose_tile(y1[:, i, :], bank).then_inc(t1_done, 1)
                elif kind == "QK":
                    if i == 0:
                        pe.wait_ge(h1_ready, upto(TPC * c + TPC))
                    g, first_head = i % HG, (NH if i < HG else 0)
                    heads = slice(first_head + 4 * g, first_head + 4 * (g + 1))
                    split_matmul(ps[:, bank, :], lambda a: wqk[:, a, heads, :].rearrange("p h w -> p (h w)"),
                                 lambda b: h1[:, b, :]).then_inc(qk_done, 1)
                elif kind == "V":
                    split_matmul(ps[:, bank, 0:C], lambda a: h1[:, a, P * i:P * (i + 1)],
                                 lambda b: wv[:, b, :]).then_inc(v_done, 1)
                elif kind == "OT":
                    pe.wait_ge(o_ready, n)
                    transpose_tile(o_sb[:, i % 2, :], bank).then_inc(ot_done, 1)
                elif kind == "PJ":
                    pe.wait_ge(ox_ready, n)
                    split_matmul(ps[:, bank, 0:C], lambda a: ox[:, i % 2, a, :],
                                 lambda b: wp[:, b, :]).then_inc(pj_done, 1)
                elif kind == "T2":
                    pe.wait_ge(y2_ready, n)
                    transpose_tile(y2[:, i, :], bank).then_inc(t2_done, 1)
                elif kind == "LG":
                    pe.wait_ge(yT_ready, n)
                    for k in range(KT):
                        rows = slice(0, P if k < KF else CR)
                        last = M(ps[:, bank, 0:E], yT[rows, i % 2, k, :], wg[rows, k, :],
                                 start=(k == 0), stop=(k == KF))
                    last.then_inc(lg_done, 1)
                elif kind == "RT":
                    pe.wait_ge(sel_ready, upto(2 * c + i + 1))
                    o = [ps[:, bank, E * k:E * (k + 1)] for k in range(3)]
                    M(o[0], before[:], r_sel[:, 0], start=True, stop=True)
                    M(o[1], before[:], r_sel[:, 1], start=True, stop=False)
                    M(o[1], ones[:], r_sel[:, 0], start=False, stop=True)
                    M(o[2], ones[:], r_sel[:, 0], start=True, stop=False)
                    M(o[2], ones[:], r_sel[:, 1], start=False, stop=True).then_inc(rt_done, 1)

            def max_scores(t, c):
                if t % TPC == 0:
                    pe.wait_ge(kblk_ready, upto(4 * (c + t // TPC) + 4))
                    pe.wait_ge(qTb_ready, upto(HG * (c + t // TPC) + HG))
                pe.wait_ge(add_done, upto(TPC * c + t))
                for g in range(HG):
                    for q in range(SEQS):
                        first = P * (t % TPC) + N * q
                        last = M(ps[N * q:N * (q + 1), g // 2, 4 * N * (g % 2):4 * N * (g % 2 + 1)],
                                 qTb[:, g, first:first + N],
                                 kblk[:, g, SEQS * (t % TPC) + q].rearrange("p i n -> p (i n)"), start=True, stop=True)
                last.then_inc(mx_done, 1)

            def move_max(t, c):
                pe.wait_ge(red_done, upto(TPC * c + t + 1))
                for g in range(HG):
                    last = nc.tensor.transpose(ps[:, 0, P * g:P * (g + 1)], mpad[:, g, :], ident[:])
                last.then_inc(mt_done, 1)

            def scores(t, c):
                pe.wait_ge(add_done, upto(TPC * c + t + 1))
                pe.wait_ge(o_ready, upto(TPC * c + t))
                for q in range(SEQS):
                    toks = slice(P * t + N * q, P * t + N * (q + 1))
                    for g in range(HG):
                        for i in range(4):
                            rows = slice(HW * i, HW * (i + 1))
                            last = M(ps[N * q:N * (q + 1), 4 + i, N * g:N * (g + 1)], kT[rows, g, toks],
                                     qT[rows, g, toks], start=True, stop=True)
                last.then_inc(st_done, 1)

            def weigh_values(t, c, half):
                if half == 0:
                    pe.wait_ge(v_ready, upto(TPC * c + t + 1))
                    wait_apart(pe, exp_done, upto(TPC * c + t + 1))
                for h in range(NH // 2 * half, NH // 2 * (half + 1)):
                    width = SEQS * VW
                    first = width * (h % (NH // 2))
                    last = M(ps[0:N, 4 + half, first:first + width], pT[:, h % 4, h // 4, :],
                             va[:, t, h].rearrange("p q d -> p (q d)"), start=True, stop=True)
                if half == 1:
                    last.then_inc(pv_done, 1)

            def chunk(c, more):
                jobs = []
                for what, name, k, bank in schedule(c, more):
                    if what == "scores":
                        scores(name, c)
                    elif what == "max":
                        max_scores(name, c)
                    elif what in ("values 0", "values 1"):
                        weigh_values(name, c, int(what[-1]))
                    elif what == "move":
                        move_max(name, c)
                    elif what == "job":
                        if not jobs:
                            pe.wait_ge(qk_read, upto(2 * HG * c + 2 * HG))
                            pe.wait_ge(v_ready, upto(TPC * c + 1))
                            pe.wait_ge(rt_read, upto(2 * c))
                        jobs.append((name, k))
                        if len(jobs) > 2:
                            wait_read(*jobs[-3])
                        job(name, k, bank)

            start_counts(pe, t1_done, qk_done, v_done, mx_done, mt_done, st_done, pv_done, ot_done, pj_done,
                         t2_done, lg_done, rt_done, t_done, s1_done, s2_done)
            done = []
            for name, c, bank in first_jobs():
                if name == ("QK", 0):
                    pe.wait_ge(wqk_ready, 1)
                if name == ("V", 0):
                    pe.wait_ge(wv_ready, 1)
                done.append((name, c))
                if len(done) > 2:
                    wait_read(*done[-3])
                job(name, c, bank)
            max_scores(0, 0)
            move_max(0, 0)
            pe.wait_ge(wp_ready, 1)
            pe.wait_ge(ld_small, 4 * 16)
            with pe.Fori(0, NC - 1) as c:
                chunk(c, True)
            chunk(NC - 1, False)

            def prepare(n):
                wait_apart(pe, ld_rows, 16 * n + 16)
                pe.wait_ge(xT_ready, upto(IT * n))
                for i in range(IT):
                    transpose_tile(xr[:, i, :], 6 + i).then_inc(t_done, 1)

            def expert(e, q):
                def item(n):
                    pe.wait_ge(xT_ready, upto(IT * n + IT))
                    for j in range(HJ):
                        pe.wait_ge(gelu_done, upto(HJ * n + max(j // 2 * 2 - 6, 0)))
                        split_matmul(unit_slot(j), lambda a: w1s[q][:, a, j, :],
                                     lambda b: xT[:, b, :]).then_inc(s1_done, 1)
                    prepare(n + 1)
                    pe.wait_ge(w2_ready, upto(2 * e + 2))
                    pe.wait_ge(y_read, upto(IT * n))
                    for i in range(IT):
                        rows = slice(P * i, P * (i + 1))
                        for j in range(HJ):
                            if i == 0:
                                pe.wait_ge(h_ready, upto(HJ * n + j + 1))
                            for k, (a, b) in enumerate(((0, 0), (0, 1), (1, 0))):
                                last = M(ps[:, 4 + i, 0:C], hs[:, a, j, rows], w2s[q][:, b, j, :],
                                         start=(j == 0 and k == 0), stop=(j == HJ - 1 and k == 2))
                        last.then_inc(s2_done, 1)

                pe.wait_ge(w1_ready, upto(e + 1))
                pe.wait_ge(w1_rest, upto(2 * e + 2))
                over_items(pe, e, item)

            prepare(0)
            with pe.Fori(0, E // 2) as e:
                expert(2 * e, 0)
                expert(2 * e + 1, 1)


_INS = ["x", "cond_1152", "L0_cond_w_adaln", "L0_cond_b_adaln", "L0_cond_w_qkv", "L0_cond_b_qkv", "L0_cond_w_proj",
        "L0_cond_b_proj", "L0_cond_w_gate", "L0_cond_w1", "L0_cond_b1", "L0_cond_w2", "L0_cond_b2"]


def kernel(**inputs):
    import numpy as _np
    import concourse.bacc as _bacc
    from concourse import mybir as _mybir
    from concourse.bass_utils import run_bass_kernel_spmd as _run

    nc = _bacc.Bacc("TRN2", target_bir_lowering=False, num_devices=1)
    arrays, args = {}, []
    for name in _INS:
        a = _np.ascontiguousarray(inputs[name])
        arrays[f"in_{name}_dram"] = a
        args.append(nc.dram_tensor(f"in_{name}_dram", a.shape, _mybir.dt.from_np(a.dtype), kind="ExternalInput").ap())
    out = nc.dram_tensor("out_dram", inputs["x"].shape, _mybir.dt.float32, kind="ExternalOutput").ap()
    adaln_moe_kernel(nc, *args, out)
    r = _run(nc, [arrays], core_ids=[0])
    return r.results[0]["out_dram"]
```
